# Optimizing a Trainium2 kernel written in Bass

```python
import numpy as np
import jax
import jax.numpy as jnp

def _softmax(x, axis=-1):
    return jax.nn.softmax(x, axis=axis)

def _gelu(x):
    return jax.nn.gelu(x, approximate=True)

def _silu(x):
    return jax.nn.silu(x)

def _sigmoid(x):
    return jax.nn.sigmoid(x)

def _layernorm(x, axis=-1, eps=1e-05):
    m = jnp.mean(x, axis=axis, keepdims=True)
    v = jnp.var(x, axis=axis, keepdims=True)
    return (x - m) / jnp.sqrt(v + eps)

def _scatter_add(tgt, idx, src, axis=0):
    return tgt.at[idx].add(src)

def _segment_sum(src, seg, n):
    return jax.ops.segment_sum(src, seg, n)
kernel_name = 'mk_macaron_d2_jaxref_r8_45e3f5'

def setup_inputs(seed: int=0):
    np.random.seed(seed)
    _w = jnp.asarray

    def _L0_attn_setup():
        import jax, jax.numpy as jnp
        import numpy as np
        B, S, D, H = (4, 256, 256, 16)
        DK = D // H
        key = jax.random.key(seed)
        ks = jax.random.split(key, 9)

        def xavier(k, shape):
            fan_in, fan_out = (shape[1], shape[0])
            limit = (6.0 / (fan_in + fan_out)) ** 0.5
            return jax.random.uniform(k, shape, jnp.float32, -limit, limit)
        return {'x': jax.random.normal(ks[0], (B, S, D), jnp.float32), 'Wq': xavier(ks[1], (D, D)), 'bq': jnp.zeros((D,), jnp.float32), 'Wk': xavier(ks[2], (D, D)), 'bk': jnp.zeros((D,), jnp.float32), 'Wv': xavier(ks[3], (D, D)), 'bv': jnp.zeros((D,), jnp.float32), 'Wo': xavier(ks[4], (D, D)), 'bo': jnp.zeros((D,), jnp.float32)}
    _L0_attn_in = _L0_attn_setup()

    def _L0_ffn_setup():
        import jax, jax.numpy as jnp
        import numpy as np
        B, S, D, FF, E = (4, 256, 256, 1024, 2)
        key = jax.random.key(seed)
        k0, k1, k2, k3, k4 = jax.random.split(key, 5)
        s = 0.02
        return {'hidden_states': jax.random.normal(k0, (B, S, D), jnp.float32), 'gate_w': jax.random.normal(k1, (E, D), jnp.float32) * s, 'w_gate': jax.random.normal(k2, (E, FF, D), jnp.float32) * s, 'w_up': jax.random.normal(k3, (E, FF, D), jnp.float32) * s, 'w_down': jax.random.normal(k4, (E, D, FF), jnp.float32) * s}
    _L0_ffn_in = _L0_ffn_setup()

    def _L1_attn_setup():
        import jax, jax.numpy as jnp
        import numpy as np
        from jax import lax
        HIDDEN = 256
        INTER = 512
        NHEADS = 64
        HEADDIM = INTER // NHEADS
        STATE = 128
        NGROUPS = 1
        CONVK = 4
        CHUNK = 32
        CONV_DIM = INTER + 2 * NGROUPS * STATE
        EPS = 1e-05
        DT_MIN, DT_MAX = (0.0, 100.0)

        def _segsum(x):
            l = x.shape[-1]
            xx = jnp.broadcast_to(x[..., None], x.shape + (l,))
            m1 = jnp.tril(jnp.ones((l, l), bool), -1)
            s = jnp.cumsum(jnp.where(m1, xx, 0.0), axis=-2)
            m2 = jnp.tril(jnp.ones((l, l), bool), 0)
            return jnp.where(m2, s, -jnp.inf)
        key = jax.random.key(seed)
        ks = jax.random.split(key, 4)
        B, S = (1, 512)
        std = 0.02
        return {'hidden_states': jax.random.normal(ks[0], (B, S, HIDDEN), jnp.float32), 'in_proj_w': jax.random.normal(ks[1], (INTER + CONV_DIM + NHEADS, HIDDEN), jnp.float32) * std, 'conv_w': jax.random.normal(ks[2], (CONV_DIM, 1, CONVK), jnp.float32) * std, 'conv_b': jnp.zeros((CONV_DIM,), jnp.float32), 'dt_bias': jnp.ones((NHEADS,), jnp.float32), 'A_log': jnp.log(jnp.arange(1, NHEADS + 1, dtype=jnp.float32)), 'D': jnp.ones((NHEADS,), jnp.float32), 'norm_w': jnp.ones((INTER,), jnp.float32), 'out_proj_w': jax.random.normal(ks[3], (HIDDEN, INTER), jnp.float32) * std}
    _L1_attn_in = _L1_attn_setup()

    def _L1_ffn_setup():
        import jax, jax.numpy as jnp
        import numpy as np
        TOP_K = 2

        def _gelu(v):
            return jax.nn.gelu(v, approximate=False)
        key = jax.random.key(seed)
        ks = jax.random.split(key, 7)
        B, T, D, I, E = (2, 256, 256, 1024, 8)
        s = 0.02
        return {'x': jax.random.normal(ks[0], (B, T, D), jnp.float32), 'rw1': jax.random.normal(ks[1], (D, D // 2), jnp.float32) * s, 'rw2': jax.random.normal(ks[2], (D // 2, E), jnp.float32) * s, 'w1': jax.random.normal(ks[3], (E, D, I), jnp.float32) * s, 'b1': jax.random.normal(ks[4], (E, I), jnp.float32) * s, 'w2': jax.random.normal(ks[5], (E, I, D), jnp.float32) * s, 'b2': jax.random.normal(ks[6], (E, D), jnp.float32) * s}
    _L1_ffn_in = _L1_ffn_setup()
    _d = {'L0_attn_x': _L0_attn_in['x'], 'L0_attn_Wq': _L0_attn_in['Wq'], 'L0_attn_bq': _L0_attn_in['bq'], 'L0_attn_Wk': _L0_attn_in['Wk'], 'L0_attn_bk': _L0_attn_in['bk'], 'L0_attn_Wv': _L0_attn_in['Wv'], 'L0_attn_bv': _L0_attn_in['bv'], 'L0_attn_Wo': _L0_attn_in['Wo'], 'L0_attn_bo': _L0_attn_in['bo'], 'L0_ffn_gate_w': _L0_ffn_in['gate_w'], 'L0_ffn_w_gate': _L0_ffn_in['w_gate'], 'L0_ffn_w_up': _L0_ffn_in['w_up'], 'L0_ffn_w_down': _L0_ffn_in['w_down'], 'L1_attn_in_proj_w': _L1_attn_in['in_proj_w'], 'L1_attn_conv_w': _L1_attn_in['conv_w'], 'L1_attn_conv_b': _L1_attn_in['conv_b'], 'L1_attn_dt_bias': _L1_attn_in['dt_bias'], 'L1_attn_A_log': _L1_attn_in['A_log'], 'L1_attn_D': _L1_attn_in['D'], 'L1_attn_norm_w': _L1_attn_in['norm_w'], 'L1_attn_out_proj_w': _L1_attn_in['out_proj_w'], 'L1_ffn_rw1': _L1_ffn_in['rw1'], 'L1_ffn_rw2': _L1_ffn_in['rw2'], 'L1_ffn_w1': _L1_ffn_in['w1'], 'L1_ffn_b1': _L1_ffn_in['b1'], 'L1_ffn_w2': _L1_ffn_in['w2'], 'L1_ffn_b2': _L1_ffn_in['b2']}
    _x0 = _d['L0_attn_x']
    _d['L0_attn_x'] = jax.random.normal(jax.random.fold_in(jax.random.key(seed), 1), (1, 1024, 256), dtype=_x0.dtype)
    del _x0
    return _d

def reference(L0_attn_x, L0_attn_Wq, L0_attn_bq, L0_attn_Wk, L0_attn_bk, L0_attn_Wv, L0_attn_bv, L0_attn_Wo, L0_attn_bo, L0_ffn_gate_w, L0_ffn_w_gate, L0_ffn_w_up, L0_ffn_w_down, L1_attn_in_proj_w, L1_attn_conv_w, L1_attn_conv_b, L1_attn_dt_bias, L1_attn_A_log, L1_attn_D, L1_attn_norm_w, L1_attn_out_proj_w, L1_ffn_rw1, L1_ffn_rw2, L1_ffn_w1, L1_ffn_b1, L1_ffn_w2, L1_ffn_b2):

    def _L0_attn_ref(x, Wq, bq, Wk, bk, Wv, bv, Wo, bo):
        import jax, jax.numpy as jnp
        import numpy as np
        B, S, D, H = (4, 256, 256, 16)
        DK = D // H
        b, s, d = x.shape
        scale = DK ** 0.5

        def proj(W, bias):
            y = jnp.einsum('bsd,ed->bse', x, W) + bias
            return y.reshape(b, s, H, DK).transpose(0, 2, 1, 3)
        Q, K, V = (proj(Wq, bq), proj(Wk, bk), proj(Wv, bv))
        scores = jnp.einsum('bhqd,bhkd->bhqk', Q, K) / scale
        causal = jnp.triu(jnp.ones((s, s), dtype=bool), k=1)
        scores = jnp.where(causal[None, None], -jnp.inf, scores)
        attn = jax.nn.softmax(scores, axis=-1)
        ctx = jnp.einsum('bhqk,bhkd->bhqd', attn, V)
        ctx = ctx.transpose(0, 2, 1, 3).reshape(b, s, d)
        out = jnp.einsum('bsd,ed->bse', ctx, Wo) + bo
        return out

    def _L0_ffn_ref(hidden_states, gate_w, w_gate, w_up, w_down):
        import jax, jax.numpy as jnp
        import numpy as np
        B, S, D, FF, E = (4, 256, 256, 1024, 2)
        b, s, d = hidden_states.shape
        x = hidden_states.reshape(-1, d)
        logits = x @ gate_w.T
        probs = jax.nn.softmax(logits.astype(jnp.float32), axis=-1)
        sel = jnp.argmax(probs, axis=-1)
        top_w = jnp.take_along_axis(probs, sel[:, None], axis=-1)
        onehot = jax.nn.one_hot(sel, gate_w.shape[0], dtype=x.dtype)
        g = jnp.einsum('td,efd->etf', x, w_gate)
        u = jnp.einsum('td,efd->etf', x, w_up)
        h = jax.nn.silu(g) * u
        y = jnp.einsum('etf,edf->etd', h, w_down)
        out = jnp.einsum('etd,te->td', y, onehot * top_w)
        return out.reshape(b, s, d)

    def _L1_attn_ref(hidden_states, in_proj_w, conv_w, conv_b, dt_bias, A_log, D, norm_w, out_proj_w):
        import jax, jax.numpy as jnp
        import numpy as np
        from jax import lax
        HIDDEN = 256
        INTER = 512
        NHEADS = 64
        HEADDIM = INTER // NHEADS
        STATE = 128
        NGROUPS = 1
        CONVK = 4
        CHUNK = 32
        CONV_DIM = INTER + 2 * NGROUPS * STATE
        EPS = 1e-05
        DT_MIN, DT_MAX = (0.0, 100.0)

        def _segsum(x):
            l = x.shape[-1]
            xx = jnp.broadcast_to(x[..., None], x.shape + (l,))
            m1 = jnp.tril(jnp.ones((l, l), bool), -1)
            s = jnp.cumsum(jnp.where(m1, xx, 0.0), axis=-2)
            m2 = jnp.tril(jnp.ones((l, l), bool), 0)
            return jnp.where(m2, s, -jnp.inf)
        Bsz, S, _ = hidden_states.shape
        proj = hidden_states @ in_proj_w.T
        gate, xBC, dt = jnp.split(proj, [INTER, INTER + CONV_DIM], axis=-1)
        xBC_t = xBC.transpose(0, 2, 1)
        xBC_t = lax.conv_general_dilated(xBC_t, conv_w, (1,), [(CONVK - 1, 0)], dimension_numbers=('NCH', 'OIH', 'NCH'), feature_group_count=CONV_DIM)
        xBC = jax.nn.silu((xBC_t + conv_b[None, :, None]).transpose(0, 2, 1))
        x, Bmat, Cmat = jnp.split(xBC, [INTER, INTER + NGROUPS * STATE], axis=-1)
        A = -jnp.exp(A_log.astype(jnp.float32))
        dt = jnp.clip(jax.nn.softplus(dt + dt_bias), DT_MIN, DT_MAX)
        x = x.reshape(Bsz, S, NHEADS, HEADDIM).astype(jnp.float32)
        Bmat = jnp.tile(Bmat.reshape(Bsz, S, NGROUPS, STATE).astype(jnp.float32), (1, 1, NHEADS // NGROUPS, 1))
        Cmat = jnp.tile(Cmat.reshape(Bsz, S, NGROUPS, STATE).astype(jnp.float32), (1, 1, NHEADS // NGROUPS, 1))
        pad = (CHUNK - S % CHUNK) % CHUNK
        D_res = D[..., None] * jnp.pad(x, ((0, 0), (0, pad), (0, 0), (0, 0)))
        x = x * dt[..., None]
        Adt = A * dt

        def chunk(t):
            t = jnp.pad(t, ((0, 0), (0, pad)) + ((0, 0),) * (t.ndim - 2))
            return t.reshape(t.shape[0], -1, CHUNK, *t.shape[2:])
        x_c, A_c, B_c, C_c = (chunk(x), chunk(Adt), chunk(Bmat), chunk(Cmat))
        A_c = A_c.transpose(0, 3, 1, 2)
        A_cum = jnp.cumsum(A_c, axis=-1)
        L = jnp.exp(_segsum(A_c))
        G = jnp.einsum('bclhn,bcshn->bclsh', C_c, B_c)
        M = G * L.transpose(0, 2, 3, 4, 1)
        Y_diag = jnp.einsum('bclsh,bcshp->bclhp', M, x_c)
        decay_states = jnp.exp(A_cum[..., -1:] - A_cum)
        B_decay = B_c * decay_states.transpose(0, 2, 3, 1)[..., None]
        states = jnp.einsum('bclhn,bclhp->bchpn', B_decay, x_c)
        states = jnp.concatenate([jnp.zeros_like(states[:, :1]), states], axis=1)
        decay_chunk = jnp.exp(_segsum(jnp.pad(A_cum[..., -1], ((0, 0), (0, 0), (1, 0)))))
        new_states = jnp.einsum('bhzj,bjhpn->bzhpn', decay_chunk, states)
        states = new_states[:, :-1]
        state_decay_out = jnp.exp(A_cum).transpose(0, 2, 3, 1)
        Y_off = jnp.einsum('bclhn,bchpn->bclhp', C_c, states) * state_decay_out[..., None]
        y = (Y_diag + Y_off).reshape(Bsz, -1, NHEADS, HEADDIM) + D_res
        y = y[:, :S].reshape(Bsz, S, INTER)
        y = y * jax.nn.silu(gate)
        var = jnp.mean(jnp.square(y), axis=-1, keepdims=True)
        y = y * lax.rsqrt(var + EPS) * norm_w
        return y @ out_proj_w.T

    def _L1_ffn_ref(x, rw1, rw2, w1, b1, w2, b2):
        import jax, jax.numpy as jnp
        import numpy as np
        TOP_K = 2

        def _gelu(v):
            return jax.nn.gelu(v, approximate=False)
        logits = _gelu(x @ rw1) @ rw2
        probs = jax.nn.softmax(logits, axis=-1)
        wgt, idx = jax.lax.top_k(probs, TOP_K)
        E = w1.shape[0]
        out = jnp.zeros_like(x)
        for e in range(E):
            Ye = _gelu(x @ w1[e] + b1[e]) @ w2[e] + b2[e]
            Ce = _gelu(b1[e]) @ w2[e] + b2[e]
            for k in range(TOP_K):
                mask = idx[..., k] == e
                active = jnp.any(mask).astype(x.dtype)
                term = jnp.where(mask[..., None], Ye, Ce)
                out = out + active * wgt[..., k:k + 1] * term
        return out
    x = L0_attn_x
    x = x + 0.5 * _L0_ffn_ref(_layernorm(x, axis=-1), L0_ffn_gate_w, L0_ffn_w_gate, L0_ffn_w_up, L0_ffn_w_down)
    x = x + _L0_attn_ref(_layernorm(x, axis=-1), L0_attn_Wq, L0_attn_bq, L0_attn_Wk, L0_attn_bk, L0_attn_Wv, L0_attn_bv, L0_attn_Wo, L0_attn_bo)
    x = x + 0.5 * _L0_ffn_ref(_layernorm(x, axis=-1), L0_ffn_gate_w, L0_ffn_w_gate, L0_ffn_w_up, L0_ffn_w_down)
    x = x + 0.5 * _L1_ffn_ref(_layernorm(x, axis=-1), L1_ffn_rw1, L1_ffn_rw2, L1_ffn_w1, L1_ffn_b1, L1_ffn_w2, L1_ffn_b2)
    x = x + _L1_attn_ref(_layernorm(x, axis=-1), L1_attn_in_proj_w, L1_attn_conv_w, L1_attn_conv_b, L1_attn_dt_bias, L1_attn_A_log, L1_attn_D, L1_attn_norm_w, L1_attn_out_proj_w)
    x = x + 0.5 * _L1_ffn_ref(_layernorm(x, axis=-1), L1_ffn_rw1, L1_ffn_rw2, L1_ffn_w1, L1_ffn_b1, L1_ffn_w2, L1_ffn_b2)
    return x

_drawn_inputs = setup_inputs


def setup_inputs(seed=0):
    import zlib

    import numpy as np

    out = dict(_drawn_inputs(seed))
    spreads = {'L0_attn_bq': (0.0, 0.703),
     'L0_attn_bk': (0.0, 0.8),
     'L0_attn_bv': (0.0, 0.1),
     'L0_attn_bo': (0.0, 0.1),
     'L1_attn_conv_b': (0.0, 0.1),
     'L1_attn_dt_bias': (1.0, 0.6),
     'L1_attn_D': (1.0, 0.2),
     'L1_attn_norm_w': (1.0, 0.2)}
    factors = {'L0_ffn_gate_w': 4.093,
     'L0_ffn_w_gate': 2.974,
     'L0_ffn_w_up': 2.944,
     'L0_ffn_w_down': 2.939,
     'L1_attn_A_log': 8.0,
     'L1_ffn_rw1': 3.971,
     'L1_ffn_rw2': 3.874,
     'L1_ffn_w1': 3.358,
     'L1_ffn_b1': 8.0,
     'L1_ffn_w2': 3.153,
     'L1_ffn_b2': 4.229}
    for name, (base, spread) in spreads.items():
        noise = np.random.default_rng([zlib.crc32(name.encode()), seed]).standard_normal(out[name].shape)
        drawn = base * np.exp(spread * noise) if base else spread * noise
        out[name] = jnp.asarray(drawn.astype(out[name].dtype))
    for name, factor in factors.items():
        out[name] = (out[name] * factor).astype(out[name].dtype)
    return out
```

```python
from contextlib import ExitStack

import concourse.bass as bass
from concourse import mybir

F32 = mybir.dt.float32
F16 = mybir.dt.float16
BF16 = mybir.dt.bfloat16
I32 = mybir.dt.int32
U32 = mybir.dt.uint32
ALU = mybir.AluOpType
ACT = mybir.ActivationFunctionType
AX = mybir.AxisListType

P = 128
T = 1024
D = 256
NT = T // P
KD = D // P
FF = 1024
CF = FF // P
E0, E1 = 2, 8
TOP1, TOP2 = 1, 2
NB0 = T * TOP1 // P + E0 - 1
NB1 = T * TOP2 // P + E1 - 1
BANK = 512
H0, DK = 16, 16
INTER, STATE, NH, HD = 512, 128, 64, 8
CONV_K = 4
EPS = 1e-5


class Count:

    def __init__(self, sem, base):
        self.sem, self.base = sem, base

    def __call__(self, value):
        return self.sem, value + self.base


class Chain:

    def __init__(self, eng, sem):
        self.eng, self.sem, self.n = eng, sem, 0

    def __call__(self, ins):
        self.n += 1
        ins.then_inc(self.sem, 1)
        self.eng.wait_ge(self.sem, self.n)


class Region:

    def __init__(self, tensor, size):
        self.tensor, self.size, self.at = tensor, size, 0

    def take(self, shape, dt, parts=P):
        n = 1
        for s in shape:
            n *= s
        width = {F32: 4, I32: 4, U32: 4, F16: 2, BF16: 2}[dt]
        size = (n * width + 31) // 32 * 32
        assert self.at + size <= self.size, ("region is full", self.at + size, self.size)
        ap = self.tensor[0:parts, self.at // 4:(self.at + size) // 4]
        if dt != F32:
            ap = ap.bitcast(dt)
        self.at += size
        ap = ap[:, 0:n]
        if len(shape) > 1:
            names = "abcd"[:len(shape)]
            ap = ap.rearrange(f"p ({' '.join(names)}) -> p {' '.join(names)}", **dict(zip(names, shape)))
        return ap


class Ctx:

    def __init__(self, nc, stack):
        self.nc, self.stack = nc, stack
        self.sems, self.counted = {}, {}

    def sem(self, name, total):
        if name not in self.sems:
            self.sems[name], self.counted[name] = self.stack.enter_context(self.nc.semaphore(name)), 0
        self.counted[name] += total
        return Count(self.sems[name], self.counted[name] - total)

    def sb(self, name, shape, dt):
        return self.stack.enter_context(self.nc.sbuf_tensor(name, shape, dt))


def layernorm_stage(c, x_done, x_count, XN):
    s_var = c.sem("ln_var", 1)
    s_sd = c.sem("ln_sd", 1)
    s_xn = c.sem("ln_xn", NT)
    s_tps = c.sem("ln_tps", NT)
    s_hi = c.sem("ln_hi", NT)
    s_lo = c.sem("ln_lo", NT)
    X, XTh, XTl = c.X, c.XTh, c.XTl
    stats, mv, veps, sd, rstd = c.ln_stats, c.ln_mv, c.ln_veps, c.ln_sd, c.ln_rstd

    def dve(eng):
        link = c.dve_link
        eng.wait_ge(*x_done(x_count))
        for t in range(NT):
            ins = eng.bn_stats(stats[:, t, :], X[:, t, :])
        link(ins)
        for t in range(NT):
            ins = eng.bn_aggr(mv[:, t, :], stats[:, t, :])
        link(ins)
        eng.tensor_scalar(veps[:, :], mv[:, :, 1], EPS, None, ALU.add).then_inc(s_var.sem, 1)
        eng.wait_ge(*s_sd(1))
        link(eng.reciprocal(rstd[:, :], sd[:, :]))
        for t in range(NT):
            eng.tensor_scalar(XN[:, t, :], X[:, t, :], mv[:, t, 0:1], rstd[:, t:t + 1],
                              ALU.subtract, ALU.mult).then_inc(s_xn.sem, 1)
        for t in range(NT):
            eng.wait_ge(*s_hi(t + 1))
            eng.tensor_tensor(XTl[:, :, t * P:(t + 1) * P], pst(t), XTh[:, :, t * P:(t + 1) * P],
                              ALU.subtract).then_inc(s_lo.sem, 1)

    def pst(t):
        return c.bank(6 + t % 2)[:, 0:D].rearrange("p (k t) -> p k t", k=KD)

    def act(eng):
        eng.wait_ge(*s_var(1))
        eng.activation(sd[:, :], veps[:, :], ACT.Sqrt).then_inc(s_sd.sem, 1)
        for t in range(NT):
            eng.wait_ge(*s_tps(t + 1))
            eng.activation(XTh[:, :, t * P:(t + 1) * P], pst(t), ACT.Copy).then_inc(s_hi.sem, 1)

    def pe(eng):
        for t in range(NT):
            eng.wait_ge(*s_xn(t + 1))
            if t >= 2:
                eng.wait_ge(*s_lo(t - 1))
            for k in range(KD):
                ins = eng.transpose(pst(t)[:, k, :], XN[:, t, k * P:(k + 1) * P], c.ident[:, :])
            ins.then_inc(s_tps.sem, 1)

    return dict(dve=dve, act=act, pe=pe, xn=s_xn, hi=s_hi, lo=s_lo)


def split_weights(c, jobs, stage, hi_engine=None, lo_engine=None, after=None):
    chunks = []
    for src, hi, lo in jobs:
        n = src.shape[1]
        w = min(n, stage.shape[2])
        for a in range(0, n, w):
            chunks.append((src, hi, lo, a, min(w, n - a)))

    n = len(chunks)
    s_in = [c.sem(("alone" if hi_engine is None else "split") + f"_in{i}", 16 * ((n + 1 - i) // 2)) for i in range(2)]
    s_hi = c.sem("split_hi", n)
    s_lo = c.sem("split_lo", n)

    def sync(eng):
        for i, (src, hi, lo, a, w) in enumerate(chunks):
            if i < 2 and after is not None:
                eng.wait_ge(*after)
            if i >= 2:
                eng.wait_ge(*s_lo(i - 1))
            eng.dma_start(stage[0:src.shape[0], i % 2, 0:w], src[:, a:a + w]).then_inc(s_in[i % 2].sem, 16)

    def hi_part(eng):
        for i, (src, hi, lo, a, w) in enumerate(chunks):
            eng.wait_ge(*s_in[i % 2](16 * (i // 2 + 1)))
            p = src.shape[0]
            if hi_engine == "act":
                ins = eng.activation(hi[:, a:a + w], stage[0:p, i % 2, 0:w], ACT.Copy)
            else:
                ins = eng.tensor_copy(hi[:, a:a + w], stage[0:p, i % 2, 0:w])
            ins.then_inc(s_hi.sem, 1)
            if hi_engine == lo_engine:
                lo_step(eng, i)

    def lo_step(eng, i):
        src, hi, lo, a, w = chunks[i]
        eng.wait_ge(*s_hi(i + 1))
        eng.tensor_tensor(lo[:, a:a + w], stage[0:src.shape[0], i % 2, 0:w], hi[:, a:a + w],
                          ALU.subtract).then_inc(s_lo.sem, 1)

    def lo_part(eng):
        for i in range(len(chunks)):
            lo_step(eng, i)

    def alone(eng, begin, end):
        if after is not None:
            eng.wait_ge(*after)
        for i in range(begin, end + 2):
            if i >= begin + 2:
                eng.wait_ge(*s_in[i % 2](16 * (i // 2)))
                src, hi, lo, a, w = chunks[i - 2]
                eng.tensor_copy(hi[:, a:a + w], stage[0:src.shape[0], i % 2, 0:w]).then_inc(s_hi.sem, 1)
                lo_step(eng, i - 2)
                eng.wait_ge(*s_lo(i - 1))
            if i < end:
                src, hi, lo, a, w = chunks[i]
                eng.dma_start(stage[0:src.shape[0], i % 2, 0:w], src[:, a:a + w]).then_inc(s_in[i % 2].sem, 16)

    if hi_engine is None:
        return dict(alone=alone, done=s_lo, count=len(chunks))
    progs = {"sync": sync, hi_engine: hi_part}
    if hi_engine != lo_engine:
        progs[lo_engine] = lo_part
    return dict(progs, done=s_lo, count=len(chunks))


def moe_stage(c, x_done, x_count, E, TOPK, NB, gated, W, region, meanwhile=None):
    XN = region.take([NT, D], F32)
    L = layernorm_stage(c, x_done, x_count, XN)
    NE = NT * E
    NYG = 4
    lg = region.take([NT, E], F32)
    sm = region.take([NT, 4], F32)
    pr = region.take([NT, E], F32)
    ex = region.take([NT, E], F32)
    cand = region.take([NT, E], F32)
    mk = [region.take([NT, E], F32) for _ in range(TOPK)]
    mk16 = [region.take([NT, E], F16) for _ in range(TOPK)]
    wk = region.take([TOPK, NT], F32)
    wkh = region.take([TOPK, NT], F32)
    slotf = region.take([TOPK, NT], F32)
    sloti = region.take([TOPK, NT], U32)
    tmp = region.take([NT, E], F32)
    full = region.take([NT, E], F32)
    cmp8 = region.take([E, NT], F32)
    nblk = region.take([4, E], F32)
    ebc = region.take([NB, E], F32)
    ebf = region.take([NB], F32)
    ebi = region.take([NB], I32)
    xg = region.take([2, D], F32)
    xgh = region.take([2, KD, P], F16)
    xgl = region.take([2, KD, P], F16)
    h = region.take([2, FF], F32)
    hTh = region.take([CF, P], F16)
    hTl = region.take([CF, P], F16)
    yo = region.take([2, D], F32)
    yg = h[:, :, :].rearrange("p a b -> p (a b)")[:, 0:NYG * D].rearrange("p (a b) -> p a b", b=D)
    if not gated:
        sel = region.take([NB], F16, parts=2 * E)
        selb = region.take([2, P], F16, parts=2 * E)
        hid = region.take([T], F32)
        coef = region.take([NT, 2 * E], F32)
        act_e = region.take([TOPK, E], F32)
        coefT = region.take([T], F32, parts=2 * E)

    n = lambda name, total: c.sem("moe_" + name, total)
    s_hid = n("hid", 0 if gated else T // BANK)
    s_hida = n("hida", 0 if gated else T // BANK)
    s_lg = n("lg", 1)
    s_d = n("d", 1)
    s_ex = n("ex", 1)
    s_mk = n("mk", 1)
    s_rk = n("rk", 1)
    s_slot = n("slot", 1)
    s_eb = n("eb", 1)
    s_sc = n("sc", 16 * NT * TOPK)
    s_xg = [n(f"xg{i}", 16 * ((NB + 1 - i) // 2)) for i in range(2)]
    s_xt = n("xt", NB)
    s_xh = n("xh", NB)
    s_xl = n("xl", NB if gated else 2 * NB)
    s_h1 = n("h1", NB)
    s_a = n("a", NB if gated else 0)
    s_h = n("h", NB)
    s_ht = n("ht", 2 * NB)
    s_hh = n("hh", 2 * NB)
    s_hl = n("hl", 2 * NB)
    s_y = n("y", NB)
    s_yo = n("yo", NB)
    s_ys = [n(f"ys{i}", 16 * ((NB + 1 - i) // 2)) for i in range(2)]
    s_yg = [n(f"yg{i}", 16 * (NT * TOPK // NYG)) for i in range(NYG)]
    s_add = n("add", NT * TOPK)
    s_xd = n("xd", NT)
    s_cf = n("cf", 0 if gated else 1)
    s_cft = n("cft", 0 if gated else 1)
    s_cfc = n("cfc", 0 if gated else T // BANK)
    s_bt = n("bt", 0 if gated else NT)
    s_bts = n("bts", 0 if gated else NT)
    HALVES = T // BANK

    def pe(eng):
        L["pe"](eng)
        for ready in W["router_ready"]:
            eng.wait_ge(*ready)
        if gated:
            eng.wait_ge(*L["lo"](NT))
            for t in range(NT):
                tok = slice(t * P, (t + 1) * P)
                i = 0
                for k in range(KD):
                    for a, b in ((c.XTh, W["gh"]), (c.XTh, W["gl"]), (c.XTl, W["gh"])):
                        ins = eng.matmul(c.bank(5)[:, t * E:(t + 1) * E], a[:, k, tok], b[:, k, :],
                                         start=(i == 0), stop=(i == 3 * KD - 1))
                        i += 1
            ins.then_inc(s_lg.sem, 1)
        else:
            for s in range(HALVES):
                eng.wait_ge(*L["lo"]((s + 1) * NT // HALVES))
                tok = slice(s * BANK, (s + 1) * BANK)
                i = 0
                for k in range(KD):
                    for a, b in ((W["r1h"], c.XTh), (W["r1l"], c.XTh), (W["r1h"], c.XTl)):
                        ins = eng.matmul(c.bank(s), a[:, k, :], b[:, k, tok], start=(i == 0), stop=(i == 3 * KD - 1))
                        i += 1
                ins.then_inc(s_hid.sem, 1)
            for t in range(NT):
                eng.wait_ge(*s_hida(t // (NT // HALVES) + 1))
                ins = eng.matmul(c.bank(5)[:, t * E:(t + 1) * E], hid[:, t * P:(t + 1) * P], W["r2"],
                                 start=True, stop=True)
            ins.then_inc(s_lg.sem, 1)
        eng.wait_ge(*s_mk(1))
        for t in range(NT):
            out = c.bank(4)[:, t * E:(t + 1) * E]
            todo = [(c.before16, k, t) for k in range(TOPK)] + [(c.ones16, k, u) for u in range(t) for k in range(TOPK)]
            for i, (m, k, u) in enumerate(todo):
                eng.matmul(out, m[:, :], mk16[k][:, u, :], start=(i == 0), stop=(i == len(todo) - 1))
        for k in range(TOPK):
            for t in range(NT):
                ins = eng.matmul(c.bank(4)[:, NE + k * E:NE + (k + 1) * E], c.ones16[:, :], mk16[k][:, t, :],
                                 start=(t == 0), stop=(t == NT - 1))
        ins.then_inc(s_rk.sem, 1)

        if not gated:
            eng.wait_ge(*s_cf(1))
            for t in range(NT):
                ins = eng.matmul(c.bank(t // 4)[0:2 * E, (t % 4) * P:(t % 4 + 1) * P], coef[:, t, :], c.ident[:, :],
                                 start=True, stop=True)
            ins.then_inc(s_cft.sem, 1)
            eng.wait_ge(*s_cfc(2))
            W["bias_pe"](eng)

        eng.wait_ge(*s_eb(1))

        def turn_x(b, p):
            eng.wait_ge(*s_xg[p](16 * (b // 2 + 1) if isinstance(b, int) else b * 8 + 16 - 8 * p))
            if not isinstance(b, int) or b > 0:
                eng.wait_ge(*s_xl(b if gated else 2 * b))
            for k in range(KD):
                ins = eng.transpose(c.bank(7)[:, k * P:(k + 1) * P], xg[:, p, k * P:(k + 1) * P], c.ident[:, :])
            ins.then_inc(s_xt.sem, 1)

        def first(b, p):
            e = eng.value_load(ebi[0:1, bass.ds(b, 1)], min_val=0, max_val=E - 1)
            eng.wait_ge(*s_xl(b + 1 if gated else 2 * b + 2))
            mats = W["first"]
            for m, (wh, wl, row) in enumerate(mats):
                for s in range(FF // BANK):
                    out = c.bank(2 * m + s) if gated else c.bank(2 * p + s)
                    i, last = 0, 3 * KD - 1 + (row is not None)
                    if row is not None:
                        eng.matmul(out, selb[:, p, :], row[:, s * BANK:(s + 1) * BANK], start=True, stop=False)
                        i = 1
                    for k in range(KD):
                        at = bass.ds(e * (KD * FF) + (k * FF + s * BANK), BANK)
                        for a, w in ((xgh, wh), (xgh, wl), (xgl, wh)):
                            ins = eng.matmul(out, a[:, p, k, :], w[:, at], start=(i == 0), stop=(i == last))
                            i += 1
            ins.then_inc(s_h1.sem, 1)

        half = CF // 2

        def turn_h(b, p):
            eng.wait_ge(*s_h(b + 1))
            for q in range(2):
                for j in range(half):
                    ins = eng.transpose(c.bank(4 + q)[:, j * P:(j + 1) * P],
                                        h[:, p, (q * half + j) * P:(q * half + j + 1) * P], c.ident[:, :])
                ins.then_inc(s_ht.sem, 1)

        def second(b, p, first_use=False):
            e = eng.value_load(ebi[0:1, bass.ds(b, 1)], min_val=0, max_val=E - 1)
            if not first_use:
                eng.wait_ge(*s_yo(b))
            w2h, w2l = W["second"]
            i = 0
            for q in range(2):
                eng.wait_ge(*s_hl(2 * b + q + 1))
                for j in range(half):
                    at = bass.ds(e * (CF * D) + (q * half + j) * D, D)
                    for a, w in ((hTh, w2h), (hTh, w2l), (hTl, w2h)):
                        ins = eng.matmul(c.bank(6)[:, 0:D], a[:, q * half + j, :], w[:, at],
                                         start=(i == 0), stop=(i == 3 * CF - 1))
                        i += 1
            ins.then_inc(s_y.sem, 1)

        for ready in W["block_ready"]:
            eng.wait_ge(*ready)
        def step(b, p, first_use=False, x=True):
            turn_h(b, p)
            first(b + 1, 1 - p)
            if x:
                turn_x(b + 2, p)
            second(b, p, first_use)

        turn_x(0, 0)
        turn_x(1, 1)
        first(0, 0)
        step(0, 0, True)
        step(1, 1)
        with eng.Fori(1, NB // 2 - 1) as i:
            step(2 * i, 0)
            step(2 * i + 1, 1)
        step(NB - 3, 0)
        step(NB - 2, 1, x=False)
        turn_h(NB - 1, 0)
        second(NB - 1, 0)
        if not gated:
            for t in range(NT):
                if t >= 2:
                    eng.wait_ge(*s_bts(t - 1))
                eng.matmul(c.bank(t % 2)[:, 0:D], coefT[:, t * P:(t + 1) * P], W["cb"], start=True, stop=True)\
                    .then_inc(s_bt.sem, 1)

    assert NB % 2 == 1

    def act(eng):
        L["act"](eng)
        if not gated:
            for s in range(HALVES):
                eng.wait_ge(*s_hid(s + 1))
                eng.activation(hid[:, s * BANK:(s + 1) * BANK], c.bank(s), ACT.Gelu).then_inc(s_hida.sem, 1)
        eng.wait_ge(*s_d(1))
        eng.activation(ex[:, :, :], lg[:, :, :], ACT.Exp).then_inc(s_ex.sem, 1)
        if not gated:
            eng.wait_ge(*s_cft(1))
            for s in range(HALVES):
                eng.activation(coefT[:, s * BANK:(s + 1) * BANK], c.bank(s)[0:2 * E, :], ACT.Copy).then_inc(s_cfc.sem, 1)
            W["bias_act"](eng)

        def block_x(b, p):
            eng.wait_ge(*s_xt(b + 1))
            eng.activation(xgh[:, p, :, :], c.bank(7)[:, 0:D].rearrange("p (k t) -> p k t", k=KD), ACT.Copy).then_inc(s_xh.sem, 1)

        def block_act(b, p):
            eng.wait_ge(*s_h1(b + 1))
            if gated:
                eng.activation(h[:, p, :], c.banks(0, 2), ACT.Silu).then_inc(s_a.sem, 1)
            else:
                eng.activation(h[:, p, :], c.banks(2 * p, 2), ACT.Gelu).then_inc(s_h.sem, 1)

        def block_h(b, p):
            for q in range(2):
                eng.wait_ge(*s_ht(2 * b + q + 1))
                eng.activation(hTh[:, q * 4:q * 4 + 4, :], c.bank(4 + q).rearrange("p (j t) -> p j t", j=4), ACT.Copy)\
                    .then_inc(s_hh.sem, 1)

        def step(b, p, x=True):
            block_h(b, p)
            block_act(b + 1, 1 - p)
            if x:
                block_x(b + 2, p)

        block_x(0, 0)
        block_x(1, 1)
        block_act(0, 0)
        with eng.Fori(0, NB // 2 - 1) as i:
            step(2 * i, 0)
            step(2 * i + 1, 1)
        step(NB - 3, 0)
        step(NB - 2, 1, x=False)
        block_h(NB - 1, 0)

    def dve(eng):
        L["dve"](eng)
        link = c.dve_link
        full3 = lambda ap: ap.unsqueeze(2).to_broadcast([P, NT, E])
        eng.wait_ge(*s_lg(1))
        lgp = c.bank(5)[:, 0:NE].rearrange("p (t e) -> p t e", e=E)
        link(eng.tensor_reduce(sm[:, :, 0], lgp, AX.X, ALU.max))
        eng.tensor_tensor(lg[:, :, :], lgp, full3(sm[:, :, 0]), ALU.subtract).then_inc(s_d.sem, 1)
        eng.wait_ge(*s_ex(1))
        link(eng.tensor_reduce(sm[:, :, 1], ex[:, :, :], AX.X, ALU.add))
        link(eng.reciprocal(sm[:, :, 2], sm[:, :, 1]))
        link(eng.tensor_tensor(pr[:, :, :], ex[:, :, :], full3(sm[:, :, 2]), ALU.mult))
        for k in range(TOPK):
            link(eng.tensor_reduce(wk[:, k, :], pr[:, :, :], AX.X, ALU.max))
            link(eng.tensor_tensor(tmp[:, :, :], pr[:, :, :], full3(wk[:, k, :]), ALU.is_equal))
            link(eng.scalar_tensor_tensor(cand[:, :, :], tmp[:, :, :], -16.0, c.iota_e[E], ALU.mult, ALU.add))
            link(eng.tensor_reduce(sm[:, :, 3], cand[:, :, :], AX.X, ALU.min))
            link(eng.tensor_tensor(mk[k][:, :, :], cand[:, :, :], full3(sm[:, :, 3]), ALU.is_equal))
            if k + 1 < TOPK:
                link(eng.scalar_tensor_tensor(pr[:, :, :], mk[k][:, :, :], -4.0, pr[:, :, :], ALU.mult, ALU.add))
        for k in range(TOPK):
            ins = eng.tensor_copy(mk16[k][:, :, :], mk[k][:, :, :])
        ins.then_inc(s_mk.sem, 1)
        link(eng.tensor_scalar(wkh[:, :, :], wk[:, :, :], 0.5, None, ALU.mult))
        eng.wait_ge(*s_rk(1))
        cnt = c.bank(4)[:, NE:NE + E]
        if TOPK == 2:
            link(eng.tensor_copy(act_e[:, 1, :], c.bank(4)[:, NE + E:NE + 2 * E]))
            link(eng.tensor_tensor(nblk[:, 3, :], cnt, act_e[:, 1, :], ALU.add))
        else:
            link(eng.tensor_copy(nblk[:, 3, :], cnt))
        link(eng.tensor_tensor(cmp8[:, :, :], nblk[:, 3, :].unsqueeze(2).to_broadcast([P, E, NT]),
                               c.step128[:, :].unsqueeze(1).to_broadcast([P, E, NT]), ALU.is_gt))
        link(eng.tensor_reduce(nblk[:, 0, :], cmp8[:, :, :], AX.X, ALU.add))
        link(eng.tensor_copy(nblk[:, 1, 0:1], nblk[:, 0, 0:1]))
        for e in range(1, E):
            link(eng.tensor_tensor(nblk[:, 1, e:e + 1], nblk[:, 1, e - 1:e], nblk[:, 0, e:e + 1], ALU.add))
        link(eng.tensor_tensor(nblk[:, 2, :], nblk[:, 1, :], nblk[:, 0, :], ALU.subtract))
        link(eng.tensor_scalar(nblk[:, 2, :], nblk[:, 2, :], float(P), None, ALU.mult))
        link(eng.tensor_tensor(full[:, :, :], c.bank(4)[:, 0:NE].rearrange("p (t e) -> p t e", e=E),
                               nblk[:, 2, :].unsqueeze(1).to_broadcast([P, NT, E]), ALU.add))
        for k in range(TOPK):
            link(eng.tensor_tensor(tmp[:, :, :], mk[k][:, :, :], full[:, :, :], ALU.mult))
            link(eng.tensor_reduce(slotf[:, k, :], tmp[:, :, :], AX.X, ALU.add))
        eng.tensor_copy(sloti[:, :, :], slotf[:, :, :]).then_inc(s_slot.sem, 1)
        link(eng.tensor_tensor(ebc[:, :, :], c.iota_b[:, 0:NB].unsqueeze(2).to_broadcast([P, NB, E]),
                               nblk[:, 1, :].unsqueeze(1).to_broadcast([P, NB, E]), ALU.is_ge))
        link(eng.tensor_reduce(ebf[:, :], ebc[:, :, :], AX.X, ALU.add))
        eng.tensor_scalar(ebi[:, :], ebf[:, :], float(E - 1), None, ALU.min).then_inc(s_eb.sem, 1)
        if not gated:
            link(eng.tensor_scalar(sel[:, :], ebf[0:2 * E, :], float(E - 1), c.row_expert[0:2 * E, :], ALU.min, ALU.is_equal))
            link(eng.tensor_copy(act_e[:, 0, :], cnt))
            link(eng.tensor_scalar(act_e[:, :, :], act_e[:, :, :], 0.5, None, ALU.is_gt))
            for k in range(TOPK):
                link(eng.tensor_scalar(tmp[:, :, :], mk[k][:, :, :], -1.0, 1.0, ALU.mult, ALU.add))
                link(eng.tensor_tensor(tmp[:, :, :], tmp[:, :, :], act_e[:, k, :].unsqueeze(1).to_broadcast([P, NT, E]), ALU.mult))
                for a, m in ((0, tmp), (E, mk[k])):
                    dst = coef[:, :, a:a + E]
                    if k == 0:
                        link(eng.tensor_tensor(dst, m[:, :, :], full3(wk[:, k, :]), ALU.mult))
                    else:
                        link(eng.tensor_tensor(cand[:, :, :], m[:, :, :], full3(wk[:, k, :]), ALU.mult))
                        link(eng.tensor_tensor(dst, dst, cand[:, :, :], ALU.add))
            eng.sem_inc(s_cf.sem, 1)
            W["bias_dve"](eng)

        def block_x(b, p):
            eng.wait_ge(*s_xh(b + 1))
            if not gated:
                eng.tensor_copy(selb[:, p, :], sel[:, bass.ds(b, 1)].to_broadcast([2 * E, P])).then_inc(s_xl.sem, 1)
            eng.tensor_tensor(xgl[:, p, :, :], c.bank(7)[:, 0:D].rearrange("p (k t) -> p k t", k=KD), xgh[:, p, :, :],
                              ALU.subtract).then_inc(s_xl.sem, 1)

        def block_gate(b, p):
            if gated:
                eng.wait_ge(*s_a(b + 1))
                eng.tensor_tensor(h[:, p, :], h[:, p, :], c.banks(2, 2), ALU.mult).then_inc(s_h.sem, 1)

        def block_h(b, p):
            for q in range(2):
                eng.wait_ge(*s_hh(2 * b + q + 1))
                eng.tensor_tensor(hTl[:, q * 4:q * 4 + 4, :], c.bank(4 + q).rearrange("p (j t) -> p j t", j=4),
                                  hTh[:, q * 4:q * 4 + 4, :], ALU.subtract).then_inc(s_hl.sem, 1)

        def block_y(b, p, first_use=False):
            eng.wait_ge(*s_y(b + 1))
            if not first_use:
                eng.wait_ge(*s_ys[p](16 * (b // 2) if isinstance(b, int) else b * 8 - 8 * p))
            eng.tensor_copy(yo[:, p, :], c.bank(6)[:, 0:D]).then_inc(s_yo.sem, 1)

        def step(b, p, first_use=False, x=True):
            block_h(b, p)
            block_gate(b + 1, 1 - p)
            if x:
                block_x(b + 2, p)
            block_y(b, p, first_use)

        block_x(0, 0)
        block_x(1, 1)
        block_gate(0, 0)
        step(0, 0, True)
        step(1, 1, True)
        with eng.Fori(1, NB // 2 - 1) as i:
            step(2 * i, 0)
            step(2 * i + 1, 1)
        step(NB - 3, 0)
        step(NB - 2, 1, x=False)
        block_h(NB - 1, 0)
        block_y(NB - 1, 0)
        for t in range(NT):
            for k in range(TOPK):
                g = t * TOPK + k
                eng.wait_ge(*s_yg[g % NYG](16 * (g // NYG + 1)))
                eng.scalar_tensor_tensor(c.X[:, t, :], yg[:, g % NYG, :], wkh[:, k, t:t + 1], c.X[:, t, :],
                                         ALU.mult, ALU.add).then_inc(s_add.sem, 1)
                eng.wait_ge(*s_add(g + 1))
            if not gated:
                eng.wait_ge(*s_bt(t + 1))
                eng.scalar_tensor_tensor(c.X[:, t, :], c.bank(t % 2)[:, 0:D], 0.5, c.X[:, t, :], ALU.mult, ALU.add)\
                    .then_inc(s_bts.sem, 1)
                eng.wait_ge(*s_bts(t + 1))
            eng.sem_inc(s_xd.sem, 1)

    def pool(eng):
        eng.wait_ge(*s_slot(1))
        eng.wait_ge(*L["xn"](NT))
        eng.wait_ge(*c.zeroed)
        for t in range(NT):
            for k in range(TOPK):
                eng.indirect_dma_start(c.xg_dram[0:NB * P, :], bass.IndirectOffsetOnAxis(ap=sloti[:, k, t:t + 1], axis=0),
                                       XN[:, t, :], None).then_inc(s_sc.sem, 16)
        if meanwhile is not None:
            meanwhile(eng)
        for p in range(2):
            eng.wait_ge(*s_ys[p](16 * ((NB + 1 - p) // 2)))
        for t in range(NT):
            for k in range(TOPK):
                g = t * TOPK + k
                if g >= NYG:
                    eng.wait_ge(*s_add(g - NYG + 1))
                eng.indirect_dma_start(yg[:, g % NYG, :], None, c.yg_dram[0:NB * P, :],
                                       bass.IndirectOffsetOnAxis(ap=sloti[:, k, t:t + 1], axis=0)).then_inc(s_yg[g % NYG].sem, 16)

    def sync(eng):
        eng.wait_ge(*s_sc(16 * NT * TOPK))

        def load(b, p, free=True):
            if free:
                eng.wait_ge(*s_xt(b - 1))
            eng.dma_start(xg[:, p, :], c.xg_dram[bass.ds(b * P, P), :]).then_inc(s_xg[p].sem, 16)

        def store(b, p):
            eng.wait_ge(*s_yo(b + 1))
            eng.dma_start(c.yg_dram[bass.ds(b * P, P), :], yo[:, p, :]).then_inc(s_ys[p].sem, 16)

        load(0, 0, False)
        load(1, 1, False)
        load(2, 0)
        with eng.Fori(0, NB // 2 - 1) as i:
            load(2 * i + 3, 1)
            store(2 * i, 0)
            load(2 * i + 4, 0)
            store(2 * i + 1, 1)
        store(NB - 3, 0)
        store(NB - 2, 1)
        store(NB - 1, 0)

    return dict(pe=pe, act=act, dve=dve, pool=pool, sync=sync, done=s_xd, count=NT)


def l1_weights(c, A, stage, w1_split, w2_stored, w1_h, w1_l, w2_h, w2_l, rr_h, rr_l, rw2, brow, cb, region, after):
    b1l = region.take([FF], F16, parts=E1)
    split = split_weights(c, [(A["b1row"], brow[0:E1, :], b1l)], stage, "pool", "pool")
    n = lambda name, total: c.sem("bias_" + name, total)
    s_in = n("in", 16 * 4)
    s_g = n("g", 1)
    s_gzh = n("gzh", 1)
    s_gz = n("gz", 1)
    s_c = n("c", 1)
    s_cb = n("cb", 1)
    s_w2 = n("w2", 16 * 2 * 2)
    s_row = n("row", 16)
    gb = region.take([E1, CF], F32)
    gz_h = region.take([E1, CF, E1], F16)
    gz_l = region.take([E1, CF, E1], F16)
    b2s = region.take([D], F32, parts=E1)
    diag = lambda ap, e: ap[:, e, :, e]

    def sync(eng):
        for w in after:
            eng.wait_ge(*w)
        eng.dma_start(rw2, A["rw2"]).then_inc(s_in.sem, 16)
        eng.dma_start(gb[:, :, :], A["b1col"].rearrange("p (e c) -> p e c", e=E1)).then_inc(s_in.sem, 16)
        eng.dma_start(b2s, A["b2"]).then_inc(s_in.sem, 16)
        eng.dma_start(cb[E1:2 * E1, :], A["b2"]).then_inc(s_in.sem, 16)
        split["sync"](eng)
        for w in w2_stored:
            eng.wait_ge(*w)
        half = w2_h.shape[1] // 2
        for a in (0, half):
            for dst, src in ((w2_h, "w2h_dram"), (w2_l, "w2l_dram")):
                eng.dma_start(dst[:, a:a + half], A[src][:, a:a + half]).then_inc(s_w2.sem, 16)
        eng.wait_ge(*split["done"](1))
        eng.dma_start(brow[E1:2 * E1, :], b1l).then_inc(s_row.sem, 16)

    def bias_act(eng):
        eng.wait_ge(*s_in(64))
        eng.activation(gb[:, :, :], gb[:, :, :], ACT.Gelu).then_inc(s_g.sem, 1)

    def bias_pe(eng):
        eng.wait_ge(*s_gz(1))
        eng.wait_ge(*s_w2(64))
        i, last = 0, 3 * E1 * CF - 1
        for e in range(E1):
            for j in range(CF):
                at = slice(e * CF * D + j * D, e * CF * D + (j + 1) * D)
                for g, w in ((gz_h, w2_h), (gz_h, w2_l), (gz_l, w2_h)):
                    ins = eng.matmul(c.bank(6)[0:E1, 0:D], g[:, e, j, :], w[:, at], start=(i == 0), stop=(i == last))
                    i += 1
        ins.then_inc(s_c.sem, 1)
        eng.wait_ge(*s_cb(1))

    def bias_dve(eng):
        link = c.dve_link
        eng.memset(gz_h[:, :, :, :], 0.0)
        link(eng.memset(gz_l[:, :, :, :], 0.0))
        eng.wait_ge(*s_g(1))
        for e in range(E1):
            ins = eng.tensor_copy(diag(gz_h, e), gb[:, e, :])
        link(ins)
        for e in range(E1):
            ins = eng.tensor_tensor(diag(gz_l, e), gb[:, e, :], diag(gz_h, e), ALU.subtract)
        ins.then_inc(s_gz.sem, 1)
        eng.wait_ge(*s_c(1))
        eng.tensor_tensor(cb[0:E1, :], c.bank(6)[0:E1, 0:D], b2s, ALU.add).then_inc(s_cb.sem, 1)

    stage_ = dict(sync=sync, pool=split["pool"])
    W = dict(r1h=rr_h, r1l=rr_l, r2=rw2, router_ready=[w1_split["done"](1), s_in(64)], first=[(w1_h, w1_l, brow)], second=(w2_h, w2_l),
             block_ready=[w1_split["done"](w1_split["count"]), s_w2(64), s_row(16)], cb=cb,
             bias_pe=bias_pe, bias_act=bias_act, bias_dve=bias_dve)
    return stage_, W


QK_ROWS = 3 * DK
W2_CHUNK = E1 * CF * D // H0
MAX_ROW = 64
NEG = -1e30
PIECES = [(k, a, min((a // BANK + 1) * BANK, T) - a) for k in range(NT)
          for a in ([k * P, BANK] if k * P < BANK else [k * P])]


def attention_weights(c, A, region):
    mats, jobs = {}, []
    for m in ("wq", "wk", "wv", "wo"):
        mats[m] = tuple(region.take([KD * D], F16) for _ in range(2))
        jobs.append((A[m], *mats[m]))
    return {m: tuple(x.rearrange("p (k e) -> p k e", k=KD) for x in v) for m, v in mats.items()}, jobs


def attention_stage(c, x_done, x_count, A, region, mats, mats_ready, stage, stage_free, before_heads):
    n = lambda name, total: c.sem("att_" + name, total)
    NP = len(PIECES)
    RING = 4
    FIRST_SCORES = 2
    LAG = 3
    XN = region.take([NT, D], F32)
    VW = DK + 1
    va = region.take([H0, NT * VW], F32)
    vcur = region.take([2, NT * VW], F32)
    qs = region.take([2, T], F16)
    ks = region.take([2, T], F16)
    at = region.at
    qk = {m: tuple(region.take([KD, T], F16) for _ in range(2)) for m in ("wq", "wk")}
    region.at = at
    pt = region.take([RING, BANK], F32)
    ct = region.take([2, T], F32, parts=VW)
    region.at = max(region.at, at + 4 * KD * T * 2)
    bias = region.take([2, KD], F32)
    bv = region.take([D], F32)
    bo = region.take([D], F32)
    mx = region.take([2, NT], F32)
    mh = region.take([2, NT], F16)
    zero = region.take([1], F16)
    zero32 = region.take([1], F32)
    w2h = region.take([2, W2_CHUNK], F16)
    w2l = region.take([2, W2_CHUNK], F16)
    maskf = region.take([2, P], F32)
    mask = region.take([2, P], BF16)
    identb = region.take([P], BF16)
    ident16 = region.take([P], F16)
    L = layernorm_stage(c, x_done, x_count, XN)
    num = pt[:, :, :].rearrange("p a b -> p (a b)").rearrange("p (k t) -> p k t", k=KD)
    den = XN[:, :, :].rearrange("p a b -> p (a b)").rearrange("p (k t) -> p k t", k=KD)

    s_c = n("c", 16 * 4)
    s_m = n("m", 1)
    s_pj = n("pj", 8)
    s_ph = n("ph", 8)
    s_pl = n("pl", 8)
    s_pd = n("pd", 16 * 12)
    s_v = n("v", NT)
    s_va = n("va", NT)
    s_ld = [n(f"ld{i}", 16 * 2 * H0 // 2) for i in range(2)]
    s_qz = n("qz", H0)
    s_vc = n("vc", H0)
    s_sm = n("sm", H0 * NT)
    s_mx = n("mx", H0 * NT)
    s_mh = n("mh", H0)
    s_mr = n("mr", H0)
    s_mc = n("mc", H0)
    s_st = n("st", H0 * NP)
    s_ex = n("ex", H0 * NP)
    s_pv = n("pv", H0 * NP)
    s_ct = n("ct", H0)
    s_cs = [n(f"cs{i}", 16 * 2 * H0 // 2) for i in range(2)]
    s_wi = [n(f"wi{i}", 16 * H0 // 2) for i in range(2)]
    s_wh = n("wh", H0)
    s_wl = n("wl", H0)
    s_ws = [n(f"ws{i}", 16 * 2 * H0 // 2) for i in range(2)]
    s_bk = n("bk", 16 * 4)
    s_nm = n("nm", KD)
    s_nh = n("nh", KD)
    s_nl = n("nl", KD)
    s_o = n("o", NT)
    s_oa = n("oa", NT)
    s_xd = n("xd", NT)
    PROJ = [(m, e, s) for m in ("wq", "wk") for e in range(KD) for s in range(T // BANK)]

    def sync(eng):
        eng.wait_ge(*x_done(x_count))
        eng.dma_start(bias[:, :, :], A["bqk"].rearrange("p (a b) -> p a b", a=2)).then_inc(s_c.sem, 16)
        eng.dma_start(bv[:, :], A["bv"]).then_inc(s_c.sem, 16)
        eng.dma_start(bo[:, :], A["bo"]).then_inc(s_c.sem, 16)
        eng.dma_start(maskf[:, :, :], A["causal"].rearrange("p (a b) -> p a b", a=2)).then_inc(s_c.sem, 16)
        for j, (m, order) in enumerate((("wq", (0, 0, 1)), ("wk", (0, 1, 0)))):
            for e in range(KD):
                eng.wait_ge(*s_pl(4 * j + 2 * e + 2))
                for g, part in enumerate(order):
                    eng.dma_start(A[m + "_dram"][g, e * P:(e + 1) * P, :], qk[m][part][:, e, :]).then_inc(s_pd.sem, 16)
        eng.wait_ge(*s_pd(16 * 12))
        eng.wait_ge(*s_m(1))

        def load(h, p, first_use=False):
            if not first_use:
                eng.wait_ge(*s_st((h - 1) * NP))
            for m, dst in (("wq", qs), ("wk", ks)):
                src = A[m + "_dram"][:, bass.ds(h * DK, DK), :]
                eng.dma_start(dst[0:QK_ROWS, p, :], src).then_inc(s_ld[p].sem, 16)

        def store(h, p):
            eng.wait_ge(*s_wl(h + 1))
            eng.wait_ge(*s_ct(h + 1))
            eng.dma_start(A["den_dram"][bass.ds(h, 1), :], ct[0:1, p, :]).then_inc(s_cs[p].sem, 16)
            eng.dma_start(A["num_dram"][bass.ds(h * DK, DK), :], ct[1:VW, p, :]).then_inc(s_cs[p].sem, 16)

        def w2_in(h, p):
            eng.dma_start(stage[:, p, :], A["w2"][:, bass.ds(h * W2_CHUNK, W2_CHUNK)]).then_inc(s_wi[p].sem, 16)

        def w2_out(h, p):
            for dst, src in (("w2h_dram", w2h), ("w2l_dram", w2l)):
                eng.dma_start(A[dst][:, bass.ds(h * W2_CHUNK, W2_CHUNK)], src[:, p, :]).then_inc(s_ws[p].sem, 16)

        load(0, 0, True)
        load(1, 1, True)
        eng.wait_ge(*stage_free)
        w2_in(0, 0)
        w2_in(1, 1)
        with eng.Fori(0, H0 // 2 - 1) as i:
            for p in range(2):
                load(2 * i + 2 + p, p)
                store(2 * i + p, p)
                w2_out(2 * i + p, p)
                w2_in(2 * i + 2 + p, p)
        for p in range(2):
            store(H0 - 2 + p, p)
            w2_out(H0 - 2 + p, p)
        for p in range(2):
            eng.wait_ge(*s_cs[p](16 * H0))
        for e in range(KD):
            eng.dma_start(num[:, e, :], A["num_dram"][e * P:(e + 1) * P, :]).then_inc(s_bk.sem, 16)
            heads = H0 // KD
            eng.dma_start(den[:, e, :], A["den_dram"][e * heads:(e + 1) * heads, :].unsqueeze(1)
                          .to_broadcast([heads, DK, T])).then_inc(s_bk.sem, 16)

    def pe(eng):
        L["pe"](eng)
        eng.wait_ge(*mats_ready)
        for j, (m, e, s) in enumerate(PROJ):
            tok = slice(s * BANK, (s + 1) * BANK)
            eng.wait_ge(*L["lo"]((s + 1) * NT // 2))
            if j >= 2:
                eng.wait_ge(*s_pl(j - 1))
            wh, wl = mats[m]
            i = 0
            for k in range(KD):
                for w, x in ((wh, c.XTh), (wl, c.XTh), (wh, c.XTl)):
                    ins = eng.matmul(c.bank(j % 2), w[:, k, e * P:(e + 1) * P], x[:, k, tok], start=(i == 0), stop=(i == 3 * KD - 1))
                    i += 1
            ins.then_inc(s_pj.sem, 1)
        wh, wl = mats["wv"]
        for t in range(NT):
            if t >= 2:
                eng.wait_ge(*s_va(t - 1))
            i = 0
            for k in range(KD):
                for x, w in ((c.XTh, wh), (c.XTh, wl), (c.XTl, wh)):
                    ins = eng.matmul(c.bank(2 + t % 2)[:, 0:D], x[:, k, t * P:(t + 1) * P], w[:, k, :],
                                     start=(i == 0), stop=(i == 3 * KD - 1))
                    i += 1
            ins.then_inc(s_v.sem, 1)
        eng.wait_ge(*s_m(1))
        eng.wait_ge(*s_va(NT))
        eng.wait_ge(*s_pl(8))

        def scores(h, p, u, first_use=False):
            slot = (p + u) % 2
            if u == 0:
                eng.wait_ge(*s_ld[p](h * 16 + 32 - 16 * p if not isinstance(h, int) else 32 * (h // 2 + 1)))
                eng.wait_ge(*s_qz(h + 1))
            if u == NT:
                eng.wait_ge(*s_mh(h + 1))
                for t in range(NT):
                    ins = eng.matmul(c.bank(2 * slot + t // 4)[MAX_ROW:MAX_ROW + 1, t % 4 * P:(t % 4 + 1) * P],
                                     mh[:, p, t:t + 1], ident16[:, :], start=True, stop=True)
                ins.then_inc(s_mr.sem, 1)
                return
            if u == 1 and not first_use:
                eng.wait_ge(*s_mc(h))
            if u >= 2:
                eng.wait_ge(*s_mx(h * NT + u - 1))
            for b in range(0, (u + 1) * P, BANK):
                w = min(BANK, (u + 1) * P - b)
                last = b + w == (u + 1) * P
                ins = eng.matmul(c.banks(2 * slot, 2)[:, b:b + w], qs[:, p, u * P:(u + 1) * P], ks[:, p, b:b + w],
                                 start=True, stop=not last)
                if last:
                    ins = eng.matmul(c.banks(2 * slot, 2)[:, u * P:(u + 1) * P], identb[:, :], mask[:, 0, :],
                                     start=False, stop=True)
            ins.then_inc(s_sm.sem, 1)

        def piece(h, p, j):
            k, a, w = PIECES[j]
            if j == 0:
                eng.wait_ge(*s_mc(h + 1))
            elif j >= 2:
                eng.wait_ge(*s_ex(h * NP + j - 1))
            out = c.bank(4 + j % 2)[:, 0:w]
            diag = a == k * P
            ins = eng.matmul(out, ks[:, p, k * P:(k + 1) * P], qs[:, p, a:a + w], start=True, stop=not diag)
            if diag:
                ins = eng.matmul(out[:, 0:P], identb[:, :], mask[:, 1, :], start=False, stop=True)
            ins.then_inc(s_st.sem, 1)

        def product(h, p, j, first_use=False):
            k, a, w = PIECES[j]
            if j == 0:
                eng.wait_ge(*s_vc(h + 1))
                if not first_use:
                    eng.wait_ge(*s_ct(h))
            eng.wait_ge(*s_ex(h * NP + j + 1))
            s = a // BANK
            eng.matmul(c.bank(6 + s)[0:VW, a - s * BANK:a - s * BANK + w], vcur[:, p, k * VW:(k + 1) * VW],
                       pt[:, j % RING, 0:w], start=(k == 0), stop=(k == (s + 1) * NT // 2 - 1)).then_inc(s_pv.sem, 1)

        def head(h, p, first_use=False, last=False):
            u = 0
            for j in range(NP + LAG):
                if j < NP:
                    piece(h, p, j)
                if not last and j >= FIRST_SCORES and u <= NT and (u < NT or j == NP):
                    scores(h + 1, 1 - p, u)
                    u += 1
                if j >= LAG:
                    product(h, p, j - LAG, first_use)
            if not last:
                assert u == NT + 1

        for u in range(NT + 1):
            scores(0, 0, u, True)
        head(0, 0, True)
        head(1, 1)
        with eng.Fori(1, H0 // 2 - 1) as i:
            head(2 * i, 0)
            head(2 * i + 1, 1)
        head(H0 - 2, 0)
        head(H0 - 1, 1, last=True)
        wh, wl = mats["wo"]
        eng.wait_ge(*s_nl(KD))
        for t in range(NT):
            if t >= 2:
                eng.wait_ge(*s_oa(t - 1))
            i = 0
            for k in range(KD):
                for x, w in ((c.XTh, wh), (c.XTh, wl), (c.XTl, wh)):
                    ins = eng.matmul(c.bank(t % 2)[:, 0:D], x[:, k, t * P:(t + 1) * P], w[:, k, :],
                                     start=(i == 0), stop=(i == 3 * KD - 1))
                    i += 1
            ins.then_inc(s_o.sem, 1)

    def act(eng):
        L["act"](eng)
        eng.wait_ge(*s_c(64))
        for j, (m, e, s) in enumerate(PROJ):
            eng.wait_ge(*s_pj(j + 1))
            b = 0 if m == "wq" else 1
            eng.activation(qk[m][0][:, e, s * BANK:(s + 1) * BANK], c.bank(j % 2), ACT.Identity, bias=bias[:, b, e:e + 1])\
                .then_inc(s_ph.sem, 1)

        def row(h, p):
            eng.wait_ge(*s_mr(h + 1))
            slot = (p + NT) % 2
            eng.activation(qs[MAX_ROW:MAX_ROW + 1, p, :], c.banks(2 * slot, 2)[MAX_ROW:MAX_ROW + 1, :], ACT.Copy)\
                .then_inc(s_mc.sem, 1)

        def head(h, p, first_use=False, last=False):
            for j, (k, a, w) in enumerate(PIECES):
                eng.wait_ge(*s_st(h * NP + j + 1))
                if not first_use or j >= RING:
                    eng.wait_ge(*s_pv(h * NP + j - RING + 1))
                eng.activation(pt[:, j % RING, 0:w], c.bank(4 + j % 2)[:, 0:w], ACT.Exp, scale=DK ** -0.5).then_inc(s_ex.sem, 1)
            if not last:
                row(h + 1, 1 - p)

        row(0, 0)
        head(0, 0, True)
        head(1, 1)
        with eng.Fori(1, H0 // 2 - 1) as i:
            head(2 * i, 0)
            head(2 * i + 1, 1)
        head(H0 - 2, 0)
        head(H0 - 1, 1, last=True)
        for k in range(KD):
            eng.wait_ge(*s_nm(k + 1))
            eng.activation(c.XTh[:, k, :], num[:, k, :], ACT.Copy).then_inc(s_nh.sem, 1)

    def dve(eng):
        L["dve"](eng)
        link = c.dve_link
        eng.wait_ge(*s_c(64))
        for i in range(2):
            eng.memset(qs[:, i, :], 0.0)
            eng.memset(ks[:, i, :], 0.0)
        va4 = va[:, :, :].rearrange("p h (t v) -> p h t v", v=VW)
        eng.memset(va4[:, :, :, 0], 1.0)
        eng.memset(zero[:, :], 0.0)
        eng.memset(zero32[:, :], 0.0)
        eng.tensor_copy(identb[:, :], c.ident[:, :])
        eng.tensor_copy(ident16[:, :], c.ident[:, :])
        link(eng.tensor_scalar(mask[:, :, :], maskf[:, :, :], NEG, None, ALU.mult))
        for i in range(2):
            ins = eng.memset(ks[MAX_ROW:MAX_ROW + 1, i, :], -1.0)
        ins.then_inc(s_m.sem, 1)
        for j, (m, e, s) in enumerate(PROJ):
            eng.wait_ge(*s_ph(j + 1))
            b = 0 if m == "wq" else 1
            tok = slice(s * BANK, (s + 1) * BANK)
            eng.scalar_tensor_tensor(qk[m][1][:, e, tok], c.bank(j % 2), bias[:, b, e:e + 1], qk[m][0][:, e, tok],
                                     ALU.add, ALU.subtract).then_inc(s_pl.sem, 1)
        for t in range(NT):
            eng.wait_ge(*s_v(t + 1))
            eng.tensor_tensor(va4[:, :, t, 1:VW], c.bank(2 + t % 2)[:, 0:D].rearrange("p (h v) -> p h v", v=DK),
                              bv[:, :].rearrange("p (h v) -> p h v", v=DK), ALU.add).then_inc(s_va.sem, 1)

        def maxima(h, p):
            for u in range(NT):
                slot = (p + u) % 2
                eng.wait_ge(*s_sm(h * NT + u + 1))
                eng.tensor_reduce(mx[:, p, u:u + 1], c.banks(2 * slot, 2)[:, 0:(u + 1) * P], AX.X, ALU.max).then_inc(s_mx.sem, 1)
            eng.wait_ge(*s_mx(h * NT + NT))
            eng.tensor_copy(mh[:, p, :], mx[:, p, :]).then_inc(s_mh.sem, 1)

        def context(h, p, first_use=False):
            eng.wait_ge(*s_pv(h * NP + NP))
            if not first_use:
                eng.wait_ge(*s_cs[p](16 * h - 16 * p))
            eng.tensor_copy(ct[:, p, :], c.banks(6, 2)[0:VW, :]).then_inc(s_ct.sem, 1)

        maxima(0, 0)
        maxima(1, 1)
        context(0, 0, True)
        maxima(2, 0)
        context(1, 1, True)
        with eng.Fori(1, H0 // 2 - 1) as i:
            maxima(2 * i + 1, 1)
            context(2 * i, 0)
            maxima(2 * i + 2, 0)
            context(2 * i + 1, 1)
        maxima(H0 - 1, 1)
        context(H0 - 2, 0)
        context(H0 - 1, 1)
        for k in range(KD):
            eng.wait_ge(*s_bk(64))
            link(eng.reciprocal(den[:, k, :], den[:, k, :]))
            eng.tensor_tensor(num[:, k, :], num[:, k, :], den[:, k, :], ALU.mult).then_inc(s_nm.sem, 1)
        for k in range(KD):
            eng.wait_ge(*s_nh(k + 1))
            eng.tensor_tensor(c.XTl[:, k, :], num[:, k, :], c.XTh[:, k, :], ALU.subtract).then_inc(s_nl.sem, 1)
        for t in range(NT):
            eng.wait_ge(*s_o(t + 1))
            eng.tensor_tensor(c.X[:, t, :], c.bank(t % 2)[:, 0:D], c.X[:, t, :], ALU.add).then_inc(s_oa.sem, 1)
            eng.wait_ge(*s_oa(t + 1))
            eng.tensor_tensor(c.X[:, t, :], c.X[:, t, :], bo[:, :], ALU.add).then_inc(s_xd.sem, 1)

    def pool(eng):
        before_heads(eng)
        eng.wait_ge(*s_m(1))
        eng.wait_ge(*s_va(NT))

        def prepare(h, p, first_use=False):
            if not first_use:
                eng.wait_ge(*s_st((h - 1) * NP))
            if not isinstance(h, int) or h > 0:
                eng.wait_ge(*s_vc(h))
            none = zero[MAX_ROW:MAX_ROW + 1, :].to_broadcast([1, T])
            eng.tensor_tensor(qs[MAX_ROW:MAX_ROW + 1, p, :], none, none, ALU.add).then_inc(s_qz.sem, 1)
            eng.wait_ge(*s_qz(h + 1))
            if not first_use:
                eng.wait_ge(*s_ct(h - 1))
            eng.tensor_copy(vcur[:, p, :], va[:, bass.ds(h, 1), :]).then_inc(s_vc.sem, 1)

        def split_w2(h, p, first_use=False):
            eng.wait_ge(*s_vc(2 if isinstance(h, int) else h + 1))
            eng.wait_ge(*s_wi[p](16 if isinstance(h, int) else h * 8 + 16 - 8 * p))
            if not first_use:
                eng.wait_ge(*s_ws[p](16 * h - 16 * p))
            eng.tensor_tensor(w2h[:, p, :], stage[:, p, :], zero32[:, :].to_broadcast([P, W2_CHUNK]), ALU.add).then_inc(s_wh.sem, 1)
            eng.wait_ge(*s_wh(h + 1))
            eng.tensor_tensor(w2l[:, p, :], stage[:, p, :], w2h[:, p, :], ALU.subtract).then_inc(s_wl.sem, 1)
            eng.wait_ge(*s_wl(h + 1))

        prepare(0, 0, True)
        prepare(1, 1, True)
        split_w2(0, 0, True)
        split_w2(1, 1, True)
        with eng.Fori(1, H0 // 2) as i:
            for p in range(2):
                prepare(2 * i + p, p)
                split_w2(2 * i + p, p)

    return dict(pe=pe, act=act, dve=dve, pool=pool, sync=sync, done=s_xd, count=NT,
                w2_stored=[s_ws[p](16 * H0) for p in range(2)])


def attention_layouts(v):
    import numpy as np
    d = {}
    for m, k in (("wq", "Wq"), ("wk", "Wk"), ("wv", "Wv"), ("wo", "Wo")):
        d[m] = v["L0_attn_" + k].T.reshape(KD, P, D).transpose(1, 0, 2).reshape(P, -1)
    d["bqk"] = np.concatenate([v["L0_attn_" + b].reshape(KD, P).T for b in ("bq", "bk")], 1)
    d["bv"] = np.tile(v["L0_attn_bv"], (P, 1))
    d["bo"] = np.tile(v["L0_attn_bo"], (P, 1))
    j = np.arange(P)
    above = (j[None, :] > j[:, None]).astype(np.float32)
    d["causal"] = np.concatenate([above, above.T], 1)
    return d


def attention_scratch():
    return dict(w2h_dram=(P, E1 * CF * D, F16), w2l_dram=(P, E1 * CF * D, F16), wq_dram=(3, H0 * DK, T, F16), wk_dram=(3, H0 * DK, T, F16), num_dram=(H0 * DK, T, F32), den_dram=(H0, T, F32))


Q = 64
NX = (INTER + 2 * STATE) // P
XC = NX * P
UNITS = 8
HU = NH // UNITS
DT_MAX = 100.0


def mixer_stage(c, x_done, x_count, A, region, region2, stage, after):
    n = lambda name, total: c.sem("mix_" + name, total)
    take, take2 = region.take, region2.take
    wo_h, wo_l = (take2([INTER // P * D], F16) for _ in range(2))
    wg_h, wg_l = (take2([KD * (INTER + NH)], F16) for _ in range(2))
    at = region2.at
    wx_h, wx_l = (take2([KD * XC], F16) for _ in range(2))
    end = region2.at
    region2.at = at
    xddh, xddl = (take2([INTER], F16) for _ in range(2))
    yT = take2([2, INTER // P, P], F16)
    S = take2([INTER], F32)
    region2.at = max(end, region2.at)
    at = region2.at
    XN = take2([NT, D], F32)
    region2.at = at
    v = take2([2, T], F32)
    th = take2([2, T], F32)
    region2.at = at
    prod = take2([2, HU * Q], F32)
    lx = take2([2, HU * Q], F32)
    mh = take2([2, HU, Q], F16)
    ml = take2([2, HU, Q], F16)
    normw = take2([INTER], F32)
    Sh, Sl = (take2([INTER], F16) for _ in range(2))
    region2.at = at + 4 * 4 * T
    bc = take([NT, 6, P], F16)
    bcs = take([6, P], F16)
    xt = take([NT, INTER], F32)
    xhl = take([2, NH, 2 * HD], F16)
    dt = take([NT, NH], F32)
    a = take([NT, NH], F32)
    ecum = take([NT, NH], F32)
    edec = take([NT, NH], F32)
    etot = take([2, NT, NH], F32)
    gm = take2([Q], F32)
    conv = take([NX, CONV_K + 1], F32)
    vec = take2([3, NH], F32)
    masks = take([4, P], F32)
    low = take2([Q], F32)
    ss = take([5], F32)
    r = dt
    e = a
    st4 = stage[:, :, :].rearrange("p a b -> p (a b)").rearrange("p (a b) -> p a b", b=INTER)
    t1, sg, yn, xf = (st4[:, i, :] for i in range(4))
    L = layernorm_stage(c, x_done, x_count, XN)
    split = split_weights(c, [(A["mix_x"], wx_h, wx_l), (A["mix_g"], wg_h, wg_l), (A["mix_o"], wo_h, wo_l)],
                          stage, "act", "dve", after=x_done(x_count))
    wx_h, wx_l = (w.rearrange("p (k n) -> p k n", k=KD) for w in (wx_h, wx_l))
    wg_h, wg_l = (w.rearrange("p (k n) -> p k n", k=KD) for w in (wg_h, wg_l))
    wo_h, wo_l = (w.rearrange("p (k n) -> p k n", k=INTER // P) for w in (wo_h, wo_l))
    U = UNITS * NT

    s_c = n("c", 16 * 4)
    s_nw = n("nw", 16)
    s_xc = n("xc", NX)
    s_cv = n("cv", NX)
    s_th = n("th", NX)
    s_si = n("si", NX)
    s_tp = n("tp", 2 * 5)
    s_tc = n("tc", 2 * 4)
    s_bh = n("bh", 3)
    s_bl = n("bl", 3)
    s_dp = n("dp", 1)
    s_dn = n("dn", 1)
    s_de = n("de", 1)
    s_dl = n("dl", 1)
    s_al = n("al", 1)
    s_a = n("aa", 1)
    s_cs = n("cs", 1)
    s_ed = n("ed", 1)
    s_bc = n("bc", NT)
    s_xd2 = n("xD", NT)
    s_pr = n("pr", U)
    s_sg = n("sg", U)
    s_lx = n("lx", U)
    s_m = n("m", U)
    s_mh = n("mh", U)
    s_ml = n("ml", U)
    s_go = n("go", U)
    s_dg = n("dg", U)
    s_xf = n("xf", NT)
    s_xh = n("xh", NT)
    s_xl = n("xl", NT)
    s_xdd = n("xdd", NT)
    s_xdh = n("xdh", NT)
    s_xdl = n("xdl", NT)
    s_g = n("g", NT)
    s_gm = n("gm", NT)
    s_gt = n("gt", NT)
    s_gth = n("gth", NT)
    s_st = n("st", 2 * NT)
    s_s = n("s", 2 * NT)
    s_sh = n("sh", 2 * NT)
    s_sl = n("sl", 2 * NT + 1)
    s_yb = n("yb", NT)
    s_y = n("y", NT)
    s_sq = n("sq", NT)
    s_v = n("v", NT)
    s_rs = n("rs", NT)
    s_yn = n("yn", NT)
    s_yt = n("yt", NT)
    s_yh = n("yh", NT)
    s_yl = n("yl", NT)
    s_o = n("o", NT)
    s_xd = n("xd", NT)

    def sync(eng):
        for w in after:
            eng.wait_ge(*w)
        eng.wait_ge(*x_done(x_count))
        for dst, name in ((conv[:, :, :], "mix_conv"), (vec[:, :, :], "mix_vec"), (masks[:, :, :], "mix_masks")):
            eng.dma_start(dst, A[name].rearrange("p (a b) -> p a b", a=dst.shape[1])).then_inc(s_c.sem, 16)
        eng.dma_start(low[:, :], A["mix_low"]).then_inc(s_c.sem, 16)
        split["sync"](eng)
        eng.wait_ge(*s_ed(1))
        eng.wait_ge(*s_bl(3))
        eng.wait_ge(*s_tc(8))
        eng.dma_start(normw[:, :], A["mix_norm"]).then_inc(s_nw.sem, 16)

    three = lambda x, w: ((x[0], w[0]), (x[0], w[1]), (x[1], w[0]))

    def pe(eng):
        L["pe"](eng)
        xT = (c.XTh, c.XTl)
        eng.wait_ge(*split["done"](split["count"]))

        def turn(ch):
            eng.wait_ge(*s_si(ch + 1))
            for q in range(2):
                i = 2 * ch + q
                if i >= 2:
                    eng.wait_ge(*s_tc(i - 1))
                for j in range(4):
                    ins = eng.transpose(c.bank(4 + q)[:, j * P:(j + 1) * P],
                                        v[:, ch % 2, (4 * q + j) * P:(4 * q + j + 1) * P], c.ident[:, :])
                ins.then_inc(s_tp.sem, 1)

        for ch in range(NX):
            if ch >= 2:
                eng.wait_ge(*s_cv(ch - 1))
            for q in range(T // BANK):
                eng.wait_ge(*L["lo"]((q + 1) * NT // 2))
                i = 0
                for k in range(KD):
                    for w, x in three((wx_h, wx_l), xT):
                        ins = eng.matmul(c.bank(2 * (ch % 2) + q), w[:, k, ch * P:(ch + 1) * P], x[:, k, q * BANK:(q + 1) * BANK],
                                         start=(i == 0), stop=(i == 3 * KD - 1))
                        i += 1
            ins.then_inc(s_xc.sem, 1)
            if ch == 0:
                for t in range(NT):
                    i = 0
                    for k in range(KD):
                        for x, w in three(xT, (wg_h, wg_l)):
                            ins = eng.matmul(c.bank(6)[:, t * NH:(t + 1) * NH], x[:, k, t * P:(t + 1) * P], w[:, k, INTER:INTER + NH],
                                             start=(i == 0), stop=(i == 3 * KD - 1))
                            i += 1
                ins.then_inc(s_dp.sem, 1)
            if ch >= 2:
                turn(ch - 2)
        turn(4)
        eng.wait_ge(*s_a(1))
        eng.wait_ge(*s_cv(NX))
        for i in range(4):
            ins = eng.matmul(c.bank(i), masks[:, i, :], a[:, :, :], start=True, stop=True)
        ins.then_inc(s_cs.sem, 1)
        eng.wait_ge(*s_ed(1))
        eng.wait_ge(*s_bl(3))

        def sums(t, u, first):
            eng.wait_ge(*s_pr(t * UNITS + u + 1))
            if not (first and u < 2):
                eng.wait_ge(*s_lx(t * UNITS + u - 1))
            eng.matmul(c.bank(u % 2), masks[:, 1, :], prod[:, u % 2, :], start=True, stop=True).then_inc(s_sg.sem, 1)

        def diagonal(t, p, u, first):
            if u == 0:
                eng.wait_ge(*s_xl(t + 1))
                if not first:
                    eng.wait_ge(*s_yb(t))
            eng.wait_ge(*s_ml(t * UNITS + u + 1))
            eng.sem_inc(s_go.sem, 1)
            for j in range(HU):
                h = u * HU + j
                for k in range(2):
                    rows = slice(k * Q, (k + 1) * Q)
                    out = c.banks(4, 2)[rows, h * 2 * HD:(h + 1) * 2 * HD]
                    eng.matmul(out, mh[rows, u % 2, j, :], xhl[rows, p, h, :], start=True, stop=False)
                    ins = eng.matmul(out[:, 0:HD], ml[rows, u % 2, j, :], xhl[rows, p, h, 0:HD], start=False, stop=True)
            ins.then_inc(s_dg.sem, 1)

        def chunk(t, k, first):
            rows = slice(k * Q, (k + 1) * Q)
            eng.wait_ge(*s_sl(2 * t + k + 1))
            for i, (x, w) in enumerate(three((bcs[:, 2, :], bcs[:, 3, :]), (Sh, Sl))):
                eng.matmul(c.bank(6)[rows, :], x[:, rows], w[:, :], start=(i == 0), stop=(i == 2))
            if k == 0:
                eng.wait_ge(*s_xdl(t + 1))
            if k == 1 and not first:
                eng.wait_ge(*s_xd(t))
            for i, (x, w) in enumerate(three((bcs[rows, 4, :], bcs[rows, 5, :]), (xddh, xddl))):
                ins = eng.matmul(c.bank(3), x, w[rows, :], start=(i == 0), stop=(i == 2))
            ins.then_inc(s_st.sem, 1)

        def output(t):
            eng.wait_ge(*s_yn(t + 1))
            for j in range(INTER // P):
                ins = eng.transpose(c.bank(7)[:, j * P:(j + 1) * P], yn[:, j * P:(j + 1) * P], c.ident[:, :])
            ins.then_inc(s_yt.sem, 1)
            eng.wait_ge(*s_yl(t + 1))
            i = 0
            for k in range(INTER // P):
                for x, w in three((yT[:, 0, :, :], yT[:, 1, :, :]), (wo_h, wo_l)):
                    ins = eng.matmul(c.bank(3)[:, 0:D], x[:, k, :], w[:, k, :], start=(i == 0), stop=(i == 3 * INTER // P - 1))
                    i += 1
            ins.then_inc(s_o.sem, 1)

        def g_matrix(t):
            eng.wait_ge(*s_bc(t + 1))
            for i, (b, w) in enumerate(three((bcs[:, 0, :], bcs[:, 1, :]), (bcs[:, 2, :], bcs[:, 3, :]))):
                ins = eng.matmul(c.bank(7)[:, 0:P], b, w, start=(i == 0), stop=(i == 2))
            ins.then_inc(s_g.sem, 1)

        def gate(t, first):
            if not first:
                eng.wait_ge(*s_y(t))
            i = 0
            for k in range(KD):
                for x, w in three(xT, (wg_h, wg_l)):
                    ins = eng.matmul(c.bank(2), x[:, k, bass.ds(t * P, P)], w[:, k, 0:INTER], start=(i == 0), stop=(i == 3 * KD - 1))
                    i += 1
            ins.then_inc(s_gt.sem, 1)
        def tile(t, p, first=False, last=False):
            if first:
                g_matrix(t)
                sums(t, 0, first)
                sums(t, 1, first)
            for u in range(UNITS):
                if u == UNITS - 1 and not last:
                    g_matrix(t + 1)
                if u + 2 < UNITS or not last:
                    sums(t, u + 2, first)
                diagonal(t, p, u, first)
                if u == 1:
                    chunk(t, 0, first)
                if u == 2:
                    gate(t, first)
                if u == 3 and not first:
                    eng.wait_ge(*s_gm(t + 1))
                    eng.wait_ge(*s_s(2 * t + 1))
                    output(t - 1)
                if u == 5:
                    chunk(t, 1, first)

        tile(0, 0, True)
        tile(1, 1)
        with eng.Fori(1, NT // 2 - 1) as i:
            tile(2 * i, 0)
            tile(2 * i + 1, 1)
        tile(NT - 2, 0)
        tile(NT - 1, 1, last=True)
        eng.wait_ge(*s_s(2 * NT))
        output(NT - 1)

    def act(eng):
        L["act"](eng)
        split["act"](eng)
        eng.wait_ge(*s_c(64))
        eng.activation(vec[:, 1, :], vec[:, 1, :], ACT.Exp).then_inc(s_al.sem, 1)
        eng.wait_ge(*s_dn(1))
        eng.activation(e[:, :, :], e[:, :, :], ACT.Exp).then_inc(s_de.sem, 1)
        eng.wait_ge(*s_de(1))
        eng.activation(e[:, :, :], e[:, :, :], ACT.Ln, bias=1.0).then_inc(s_dl.sem, 1)
        tiles = lambda i: bc[:, :, i, :]

        def turned(ch):
            for q in range(2):
                eng.wait_ge(*s_tp(2 * ch + q + 1))
                src = c.bank(4 + q).rearrange("p (t n) -> p t n", t=4)
                if ch < 4:
                    eng.activation(xt[:, 4 * q:4 * q + 4, ch * P:(ch + 1) * P], src, ACT.Copy).then_inc(s_tc.sem, 1)
                else:
                    ins = eng.activation(bc[:, 4 * q:4 * q + 4, 4, :], src, ACT.Copy)
                    if q == 1:
                        ins.then_inc(s_bh.sem, 1)

        for ch in range(NX):
            eng.wait_ge(*s_cv(ch + 1))
            if ch >= 2:
                eng.wait_ge(*s_si(ch - 1))
            eng.activation(th[:, ch % 2, :], v[:, ch % 2, :], ACT.Tanh).then_inc(s_th.sem, 1)
            if ch >= 2 and ch < 6:
                turned(ch - 2)
        for i, ch in enumerate((4, 5)):
            eng.wait_ge(*s_si(ch + 1))
            eng.activation(tiles(2 * i), v[:, ch % 2, :].rearrange("p (t n) -> p t n", t=NT), ACT.Copy).then_inc(s_bh.sem, 1)
        turned(4)
        eng.wait_ge(*s_cs(1))
        eng.activation(ecum[:, :, :], c.bank(0).rearrange("p (t h) -> p t h", h=NH), ACT.Exp)
        eng.activation(edec[:, :, :], c.bank(1).rearrange("p (t h) -> p t h", h=NH), ACT.Exp)
        eng.activation(etot[:, :, :, :].rearrange("p c t h -> p (c t h)"), c.banks(2, 2), ACT.Exp).then_inc(s_ed.sem, 1)
        eng.wait_ge(*s_bl(3))

        def decays(t, u, first):
            eng.wait_ge(*s_sg(t * UNITS + u + 1))
            if not (first and u < 2):
                eng.wait_ge(*s_ml(t * UNITS + u - 1))
            eng.activation(lx[:, u % 2, :], c.bank(u % 2), ACT.Exp).then_inc(s_lx.sem, 1)

        def m_hi(t, u, first):
            eng.wait_ge(*s_m(t * UNITS + u + 1))
            if not (first and u < 2):
                eng.wait_ge(*s_dg(t * UNITS + u - 1))
            eng.activation(mh[:, u % 2, :, :].rearrange("p h l -> p (h l)"), lx[:, u % 2, :], ACT.Copy).then_inc(s_mh.sem, 1)

        def state(t, k):
            eng.wait_ge(*s_s(2 * t + k + 1))
            eng.activation(Sh[:, :], S[:, :], ACT.Copy).then_inc(s_sh.sem, 1)

        def y_hi(t):
            eng.wait_ge(*s_yt(t + 1))
            eng.activation(yT[:, 0, :, :], c.bank(7).rearrange("p (k t) -> p k t", t=P), ACT.Copy).then_inc(s_yh.sem, 1)

        def squares(t):
            eng.wait_ge(*s_y(t + 1))
            eng.activation(sg, t1, ACT.Square, scale=INTER ** -0.5, accum_out=ss[:, 0:1]).then_inc(s_sq.sem, 1)

        def x_hi(t, p):
            eng.wait_ge(*s_xf(t + 1))
            eng.activation(xhl[:, p, :, 0:HD], xf.rearrange("p (h d) -> p h d", d=HD), ACT.Copy).then_inc(s_xh.sem, 1)

        def tile(t, p, first=False, last=False):
            if first:
                x_hi(t, p)
                decays(t, 0, first)
            eng.wait_ge(*s_xdd(t + 1))
            eng.activation(xddh[:, :], xf, ACT.Copy).then_inc(s_xdh.sem, 1)
            for u in range(UNITS):
                if u + 1 < UNITS or not last:
                    decays(t, u + 1, first)
                m_hi(t, u, first)
                if u == 1 and not first:
                    squares(t - 1)
                if u == 2:
                    state(t, 0)
                if u == 4 and not first:
                    y_hi(t - 1)
                if u == 5 and not last:
                    x_hi(t + 1, 1 - p)
                if u == 6:
                    state(t, 1)
                    eng.wait_ge(*s_gt(t + 1))
                    eng.activation(sg, c.bank(2), ACT.Tanh, scale=0.5).then_inc(s_gth.sem, 1)

        tile(0, 0, True)
        tile(1, 1)
        with eng.Fori(1, NT // 2 - 1) as i:
            tile(2 * i, 0)
            tile(2 * i + 1, 1)
        tile(NT - 2, 0)
        tile(NT - 1, 1, last=True)
        squares(NT - 1)
        y_hi(NT - 1)

    def dve(eng):
        L["dve"](eng)
        split["dve"](eng)
        link = c.dve_link
        eng.wait_ge(*s_c(64))
        link(eng.tensor_scalar(conv[:, :, :], conv[:, :, :], 0.5, None, ALU.mult))
        over_t = lambda i: vec[:, i, :].unsqueeze(1).to_broadcast([P, NT, NH])

        def convolve(ch):
            eng.wait_ge(*s_xc(ch + 1))
            ps = c.banks(2 * (ch % 2), 2)
            if ch >= 2:
                if ch - 2 < 4:
                    eng.wait_ge(*s_tp(2 * (ch - 2) + 2))
            link(eng.tensor_scalar(v[:, ch % 2, :], ps, conv[:, ch, CONV_K - 1:CONV_K], conv[:, ch, CONV_K:CONV_K + 1],
                                   ALU.mult, ALU.add))
            for k in range(CONV_K - 2, -1, -1):
                back = CONV_K - 1 - k
                ins = eng.scalar_tensor_tensor(v[:, ch % 2, back:T], ps[:, 0:T - back], conv[:, ch, k:k + 1],
                                               v[:, ch % 2, back:T], ALU.mult, ALU.add)
                if k:
                    link(ins)
            ins.then_inc(s_cv.sem, 1)

        def silu(ch):
            eng.wait_ge(*s_th(ch + 1))
            eng.scalar_tensor_tensor(v[:, ch % 2, :], th[:, ch % 2, :], 1.0, v[:, ch % 2, :], ALU.add, ALU.mult)\
                .then_inc(s_si.sem, 1)

        convolve(0)
        eng.wait_ge(*s_dp(1))
        link(eng.tensor_tensor(r[:, :, :], c.bank(6).rearrange("p (t h) -> p t h", h=NH), over_t(0), ALU.add))
        eng.scalar_tensor_tensor(e[:, :, :], r[:, :, :], -1.0, r[:, :, :], ALU.mult, ALU.min).then_inc(s_dn.sem, 1)
        convolve(1)
        silu(0)
        eng.wait_ge(*s_dl(1))
        link(eng.scalar_tensor_tensor(dt[:, :, :], r[:, :, :], 0.0, e[:, :, :], ALU.max, ALU.add))
        link(eng.tensor_scalar(dt[:, :, :], dt[:, :, :], 0.0, DT_MAX, ALU.max, ALU.min))
        eng.wait_ge(*s_al(1))
        eng.scalar_tensor_tensor(a[:, :, :], dt[:, :, :], -1.0, over_t(1), ALU.mult, ALU.mult).then_inc(s_a.sem, 1)
        for ch in range(2, NX):
            convolve(ch)
            silu(ch - 1)
        for i, ch in enumerate((4, 5)):
            if ch == 5:
                silu(5)
            eng.wait_ge(*s_bh(i + 1))
            eng.tensor_tensor(bc[:, :, 2 * i + 1, :], v[:, ch % 2, :].rearrange("p (t n) -> p t n", t=NT), bc[:, :, 2 * i, :],
                              ALU.subtract).then_inc(s_bl.sem, 1)
        eng.wait_ge(*s_bh(3))
        for q in range(2):
            ins = eng.tensor_tensor(bc[:, 4 * q:4 * q + 4, 5, :], c.bank(4 + q).rearrange("p (t n) -> p t n", t=4),
                                    bc[:, 4 * q:4 * q + 4, 4, :], ALU.subtract)
        ins.then_inc(s_bl.sem, 1)
        eng.wait_ge(*s_bl(3))
        eng.wait_ge(*s_tp(10))
        eng.memset(ss[:, 3:4], -0.5)
        eng.memset(ss[:, 4:5], EPS)
        eng.memset(S[:, :], 0.0)
        eng.memset(Sh[:, :], 0.0)
        eng.memset(Sl[:, :], 0.0).then_inc(s_sl.sem, 1)
        eng.wait_ge(*s_ed(1))
        eng.wait_ge(*s_sl(1))
        heads = lambda ap: ap.rearrange("p (h d) -> p h d", d=HD)
        per_head = lambda ap, t: ap[:, bass.ds(t, 1), :].rearrange("p o h -> p (o h)").unsqueeze(2).to_broadcast([P, NH, HD])

        def dt_x(t, p):
            x = xt[:, bass.ds(t, 1), :].rearrange("p o (h d) -> p (o h) d", d=HD)
            eng.tensor_tensor(heads(xf), x, per_head(dt, t), ALU.mult).then_inc(s_xf.sem, 1)
            eng.wait_ge(*s_xh(t + 1))
            eng.tensor_tensor(xhl[:, p, :, HD:], heads(xf), xhl[:, p, :, 0:HD], ALU.subtract).then_inc(s_xl.sem, 1)

        def decay_x(t, first):
            eng.wait_ge(*s_xl(t + 1))
            if not first:
                eng.wait_ge(*s_st(2 * t))
            eng.tensor_tensor(heads(xf), heads(xf), per_head(edec, t), ALU.mult).then_inc(s_xdd.sem, 1)
            eng.wait_ge(*s_xdh(t + 1))
            eng.tensor_tensor(xddl[:, :], xf, xddh[:, :], ALU.subtract).then_inc(s_xdl.sem, 1)

        def times_g(t, u):
            eng.wait_ge(*s_lx(t * UNITS + u + 1))
            x = lx[:, u % 2, :].rearrange("p (h l) -> p h l", l=Q)
            eng.tensor_tensor(x, x, gm[:, :].unsqueeze(1).to_broadcast([P, HU, Q]), ALU.mult).then_inc(s_m.sem, 1)

        def m_lo(t, u, first):
            eng.wait_ge(*s_mh(t * UNITS + u + 1))
            eng.tensor_tensor(ml[:, u % 2, :, :].rearrange("p h l -> p (h l)"), lx[:, u % 2, :],
                              mh[:, u % 2, :, :].rearrange("p h l -> p (h l)"), ALU.subtract).then_inc(s_ml.sem, 1)

        def state(t, k):
            tot = etot[:, k, bass.ds(t, 1), :].rearrange("p o h -> p (o h)").unsqueeze(2).to_broadcast([P, NH, HD])
            eng.tensor_tensor(heads(S), heads(S), tot, ALU.mult).then_inc(s_stx.sem, 1)
            eng.wait_ge(*s_stx(2 * t + k + 1))
            eng.wait_ge(*s_st(2 * t + k + 1))
            eng.tensor_tensor(S[:, :], S[:, :], c.bank(3), ALU.add).then_inc(s_s.sem, 1)
            eng.wait_ge(*s_sh(2 * t + k + 1))
            eng.tensor_tensor(Sl[:, :], S[:, :], Sh[:, :], ALU.subtract).then_inc(s_sl.sem, 1)

        def combine(t):
            yd = c.banks(4, 2).rearrange("p (h e) -> p h e", e=2 * HD)
            eng.wait_ge(*s_st(2 * t + 2))
            eng.wait_ge(*s_yk(6 * t + 1))
            eng.tensor_tensor(heads(t1), heads(c.bank(6)), per_head(ecum, t), ALU.mult).then_inc(s_yk.sem, 1)
            eng.wait_ge(*s_gth(t + 1))
            eng.scalar_tensor_tensor(sg, sg, 1.0, c.bank(2), ALU.add, ALU.mult).then_inc(s_yk.sem, 1)
            eng.wait_ge(*s_yk(6 * t + 2))
            eng.wait_ge(*s_xd2(t + 1))
            eng.tensor_tensor(t1, t1, xt[:, bass.ds(t, 1), :].rearrange("p o n -> p (o n)"), ALU.add).then_inc(s_yk.sem, 1)
            eng.wait_ge(*s_yk(6 * t + 4))
            eng.wait_ge(*s_dg(t * UNITS + UNITS))
            eng.tensor_tensor(heads(t1), heads(t1), yd[:, :, 0:HD], ALU.add).then_inc(s_yk.sem, 1)
            eng.wait_ge(*s_yk(6 * t + 5))
            eng.tensor_tensor(heads(t1), heads(t1), yd[:, :, HD:], ALU.add).then_inc(s_yb.sem, 1)
            eng.wait_ge(*s_yb(t + 1))
            eng.sem_inc(s_yk.sem, 1)
            eng.wait_ge(*s_yk(6 * t + 6))
            eng.scalar_tensor_tensor(t1, t1, 0.5, sg, ALU.mult, ALU.mult).then_inc(s_y.sem, 1)
            eng.sem_inc(s_yk.sem, 1)

        def normalise(t):
            eng.wait_ge(*s_rs(t + 1))
            eng.scalar_tensor_tensor(yn, t1, ss[:, 2:3], normw, ALU.mult, ALU.mult).then_inc(s_yn.sem, 1)

        def output(t):
            eng.wait_ge(*s_yh(t + 1))
            eng.tensor_tensor(yT[:, 1, :, :], c.bank(7).rearrange("p (k t) -> p k t", t=P), yT[:, 0, :, :], ALU.subtract)\
                .then_inc(s_yl.sem, 1)
            eng.wait_ge(*s_o(t + 1))
            x = c.X[:, bass.ds(t, 1), :].rearrange("p o d -> p (o d)")
            eng.tensor_tensor(x, x, c.bank(3)[:, 0:D], ALU.add).then_inc(s_xd.sem, 1)

        def g_masked(t):
            eng.wait_ge(*s_g(t + 1))
            for k in range(2):
                rows = slice(k * Q, (k + 1) * Q)
                ins = eng.tensor_tensor(gm[rows, :], c.bank(7)[rows, k * Q:(k + 1) * Q], low[rows, :], ALU.mult)
            ins.then_inc(s_gm.sem, 1)
            eng.wait_ge(*s_gm(t + 1))

        def tile(t, p, first=False, last=False):
            if first:
                dt_x(t, p)
            decay_x(t, first)
            if first:
                g_masked(t)
                times_g(t, 0)
            for u in range(UNITS):
                if u == UNITS - 1 and not last:
                    g_masked(t + 1)
                if u + 1 < UNITS or not last:
                    times_g(t, u + 1)
                m_lo(t, u, first)
                if u == 2:
                    state(t, 0)
                if u == 3 and not first:
                    normalise(t - 1)
                if u == 4 and not first:
                    output(t - 1)
                if u == 5 and not last:
                    dt_x(t + 1, 1 - p)
                if u == 6:
                    state(t, 1)
            combine(t)

        eng.sem_inc(s_yk.sem, 1)
        eng.wait_ge(*s_nw(16))
        tile(0, 0, True)
        tile(1, 1)
        with eng.Fori(1, NT // 2 - 1) as i:
            tile(2 * i, 0)
            tile(2 * i + 1, 1)
        tile(NT - 2, 0)
        tile(NT - 1, 1, last=True)
        normalise(NT - 1)
        output(NT - 1)

    s_stx = n("stx", 2 * NT)
    s_yk = n("yk", 6 * NT + 1)

    def pool(eng):
        eng.wait_ge(*s_ed(1))
        eng.wait_ge(*s_bl(3))
        eng.wait_ge(*s_sl(1))
        heads = lambda ap: ap.rearrange("p (h d) -> p h d", d=HD)

        def rstd(t):
            eng.wait_ge(*s_sq(t + 1))
            eng.tensor_tensor(ss[:, 1:2], ss[:, 0:1], ss[:, 4:5], ALU.add).then_inc(s_v.sem, 1)
            eng.wait_ge(*s_v(t + 1))
            eng.tensor_tensor(ss[:, 2:3], ss[:, 1:2], ss[:, 3:4], ALU.pow).then_inc(s_rs.sem, 1)

        def tile(t, p, first=False):
            if not first:
                eng.wait_ge(*s_st(2 * t))
            flat = bc[:, bass.ds(t, 1), :, :].rearrange("p o a b -> p (o a b)").bitcast(F32)
            eng.tensor_copy(bcs[:, :, :].rearrange("p a b -> p (a b)").bitcast(F32), flat).then_inc(s_bc.sem, 1)
            for u in range(UNITS):
                if not (first and u < 2):
                    eng.wait_ge(*s_sg(t * UNITS + u - 1))
                x = a[:, bass.ds(t, 1), u * HU:(u + 1) * HU].rearrange("p o h -> p (o h)").unsqueeze(2).to_broadcast([P, HU, Q])
                eng.tensor_tensor(prod[:, u % 2, :].rearrange("p (h l) -> p h l", l=Q), x,
                                  low[:, :].unsqueeze(1).to_broadcast([P, HU, Q]), ALU.mult).then_inc(s_pr.sem, 1)
                if u == 2 and not first:
                    rstd(t - 1)
                if u == 3:
                    x = xt[:, bass.ds(t, 1), :].rearrange("p o (h d) -> p (o h) d", d=HD)
                    eng.wait_ge(*s_xf(t + 1))
                    eng.tensor_tensor(x, x, vec[:, 2, :].unsqueeze(2).to_broadcast([P, NH, HD]), ALU.mult).then_inc(s_xd2.sem, 1)

        tile(0, 0, True)
        tile(1, 1)
        with eng.Fori(1, NT // 2) as i:
            tile(2 * i, 0)
            tile(2 * i + 1, 1)
        rstd(NT - 1)

    return dict(pe=pe, act=act, dve=dve, pool=pool, sync=sync, done=s_xd, count=NT)


def mixer_layouts(v):
    import numpy as np
    w = v["L1_attn_in_proj_w"]
    cols = lambda m: m.T.reshape(KD, P, -1).transpose(1, 0, 2).reshape(P, -1)
    j = np.arange(P)
    same = j[:, None] // Q == j[None, :] // Q
    row = lambda x: np.tile(x.reshape(1, -1), (P, 1))
    f = lambda m: m.astype(np.float32)
    return dict(
        mix_g=cols(np.concatenate([w[:INTER], w[INTER + XC:]])),
        mix_x=cols(w[INTER:INTER + XC]),
        mix_o=v["L1_attn_out_proj_w"].T.reshape(INTER // P, P, D).transpose(1, 0, 2).reshape(P, -1),
        mix_conv=np.concatenate([v["L1_attn_conv_w"].reshape(NX, P, CONV_K), v["L1_attn_conv_b"].reshape(NX, P, 1)], 2)
        .transpose(1, 0, 2).reshape(P, -1),
        mix_vec=np.concatenate([row(v["L1_attn_dt_bias"]), row(v["L1_attn_A_log"]), row(v["L1_attn_D"])], 1),
        mix_norm=row(v["L1_attn_norm_w"]),
        mix_masks=np.concatenate([f(same & (j[:, None] <= j[None, :])), f(same & (j[:, None] > j[None, :])),
                                  f(np.tile(j[:, None] < Q, (1, P))), f(np.tile(j[:, None] >= Q, (1, P)))], 1),
        mix_low=f((j % Q)[:, None] <= np.arange(Q)[None, :]),
    )



W1_FIRST = 14


def program(nc, A, out, stages="fafmsm"):
    with ExitStack() as stack:
        c = Ctx(nc, stack)
        psum = stack.enter_context(nc.psum_tensor("psum", [P, 8 * BANK], F32))
        c.bank = lambda i: psum[:, i * BANK:(i + 1) * BANK]
        c.banks = lambda i, n: psum[:, i * BANK:(i + n) * BANK]
        c.X = c.sb("X", [P, NT, D], F32)
        c.XTh = c.sb("XTh", [P, KD, T], F16)
        c.XTl = c.sb("XTl", [P, KD, T], F16)
        c.ident = c.sb("ident", [P, P], F32)
        c.before16 = c.sb("before16", [P, P], F16)
        c.ones16 = c.sb("ones16", [P, P], F16)
        iota = c.sb("iota", [P, NT * E0 + NT * E1 + 32 + NT + 1], F32)
        a = NT * E0
        b = a + NT * E1
        c.iota_e = {E0: iota[:, 0:a].rearrange("p (t e) -> p t e", e=E0), E1: iota[:, a:b].rearrange("p (t e) -> p t e", e=E1)}
        c.iota_b = iota[:, b:b + 32]
        c.step128 = iota[:, b + 32:b + 32 + NT]
        c.row_expert = iota[:, b + 32 + NT:b + 33 + NT]
        c.ln_stats = c.sb("ln_stats", [P, NT, 6], F32)
        c.ln_mv = c.sb("ln_mv", [P, NT, 2], F32)
        c.ln_veps = c.sb("ln_veps", [P, NT], F32)
        c.ln_sd = c.sb("ln_sd", [P, NT], F32)
        c.ln_rstd = c.sb("ln_rstd", [P, NT], F32)
        stage = c.sb("stage", [P, 2, 1024], F32)
        small = c.sb("small", [P, 512], F32)
        smallr = Region(small, 2048)
        size0 = 4 * 3 * E0 * KD * FF + 2048 + 672
        mem0 = c.sb("mem0", [P, size0 // 4], F32)
        mem1 = c.sb("mem1", [P, E1 * KD * FF], F32)
        mem2 = c.sb("mem2", [P, E1 * CF * D], F32)
        s_const = c.sem("const", 48)
        s_x = c.sem("x_loaded", 16 * NT)
        s_zero = c.sem("xg_zeroed", 16)
        s_z = c.sem("zeros_made", 3)
        s_out = c.sem("stored", 16 * NT)
        s_link = c.sem("dve_link", 0)
        c.zeroed = s_zero(16)
        c.xg_dram = A["xg_dram"]
        c.yg_dram = A["yg_dram"]

        r0 = Region(mem0, size0)
        gate_h, gate_l, up_h, up_l, down_h, down_l = (r0.take([E0 * KD * FF], F16) for _ in range(6))
        rg_h, rg_l = (smallr.take([KD, E0], F16) for _ in range(2))
        r1 = Region(mem1, 4 * E1 * KD * FF)
        w1_h, w1_l = (r1.take([E1 * KD * FF], F16) for _ in range(2))
        r2 = Region(mem2, 4 * E1 * CF * D)
        w2_h, w2_l = (r2.take([E1 * CF * D], F16) for _ in range(2))
        rr_h, rr_l = (smallr.take([KD, P], F16) for _ in range(2))
        rw2 = smallr.take([E1], F32)

        flat = lambda ap: ap.rearrange("p a b -> p (a b)")
        mats_r = Region(mem2, 4 * E1 * CF * D)
        mats_r.at = mats_r.size - 4 * KD * D * 4
        mats_at = mats_r.at
        mats, mat_jobs = attention_weights(c, A, mats_r)
        split0 = split_weights(c, [(A["gate"], rg_h.rearrange("p a b -> p (a b)"), rg_l.rearrange("p a b -> p (a b)")),
                                         (A["w_gate"], gate_h, gate_l), (A["w_up"], up_h, up_l),
                                         (A["w_down"], down_h, down_l), *mat_jobs], stage, "act", "dve")
        progs = [split0]
        W0 = dict(gh=rg_h, gl=rg_l, router_ready=[split0["done"](1)], first=[(gate_h, gate_l, None), (up_h, up_l, None)],
                  second=(down_h, down_l), block_ready=[split0["done"](split0["count"] - 4)])

        split1 = split_weights(c, [(A["rw1"], flat(rr_h), flat(rr_l)), (A["w1"], w1_h, w1_l)], stage,
                               after=split0["done"](split0["count"]))

        done, count = s_x, 16 * NT
        mixer_at = 0
        n_l0, n_l1 = 0, 0
        l1_ready = False
        for n, kind in enumerate(stages):
            if kind == "f":
                st = moe_stage(c, done, count, E0, TOP1, NB0, True, W0, Region(mem2, mats_at),
                               (lambda eng: split1["alone"](eng, 0, W1_FIRST)) if n == 0 else None)
            elif kind == "m":
                if not l1_ready:
                    l1_ready = True
                    keep = Region(mem0, size0)
                    brow = keep.take([FF], F16, parts=2 * E1)
                    cb = keep.take([D], F32, parts=2 * E1)
                    mixer_at = keep.at
                    weights, W1 = l1_weights(c, A, stage, split1, w2_stored, w1_h, w1_l, w2_h, w2_l, rr_h, rr_l, rw2, brow, cb, keep,
                                             [done(count), split1["done"](split1["count"])])
                    progs.append(weights)
                    l1_at = keep.at
                reg = Region(mem0, size0)
                reg.at = l1_at
                st = moe_stage(c, done, count, E1, TOP2, NB1, False, W1, reg)
                W1 = dict(W1, bias_pe=lambda e: None, bias_act=lambda e: None, bias_dve=lambda e: None)
            elif kind == "a":
                st = attention_stage(c, done, count, A, Region(mem2, mats_at), mats, split0["done"](split0["count"]),
                                     stage, split1["done"](split1["count"]),
                                     lambda eng: split1["alone"](eng, W1_FIRST, split1["count"]))
                w2_stored = st["w2_stored"]
            elif kind == "s":
                reg = Region(mem0, size0)
                reg.at = mixer_at
                half = Region(mem2, 4 * E1 * CF * D)
                half.at = half.size // 2
                st = mixer_stage(c, done, count, A, reg, half, stage, [split1["done"](split1["count"])])
            progs.append(st)
            if kind == "s" and l1_ready:
                s_back = c.sem("w2l_back", 16)

                def back(eng, mixed=st["done"](st["count"])):
                    eng.wait_ge(*mixed)
                    eng.dma_start(w2_l, A["w2l_dram"]).then_inc(s_back.sem, 16)
                progs.append(dict(sync=back))
                W1 = dict(W1, block_ready=W1["block_ready"] + [s_back(16)])
            done, count = st["done"], st["count"]

        with nc.Block() as block:
            @block.sync
            def _(eng):
                for t in range(NT):
                    eng.dma_start(c.X[:, t, :], A["x"][t * P:(t + 1) * P, :]).then_inc(s_x.sem, 16)
                eng.dma_start(c.ident[:, :], A["ident"]).then_inc(s_const.sem, 16)
                eng.dma_start(iota[:, :], A["iota"]).then_inc(s_const.sem, 16)
                eng.dma_start(stage[:, 0, 0:P], A["before"]).then_inc(s_const.sem, 16)
                eng.wait_ge(*s_z(3))
                zero = mem1[:, 0:NB1 * D].rearrange("p (b d) -> p b d", d=D)
                eng.dma_start(A["xg_dram"].rearrange("(b p) d -> p b d", p=P), zero).then_inc(s_zero.sem, 16)
                for g in progs:
                    if "sync" in g:
                        g["sync"](eng)
                for t in range(NT):
                    eng.wait_ge(*done(count - NT + t + 1))
                    eng.dma_start(out[t * P:(t + 1) * P, :], c.X[:, t, :]).then_inc(s_out.sem, 16)
                eng.wait_ge(*s_out(16 * NT))

            @block.scalar
            def _(eng):
                for g in progs:
                    if "act" in g:
                        g["act"](eng)

            @block.vector
            def _(eng):
                eng.memset(mem1[:, 0:NB1 * D], 0.0).then_inc(s_z.sem, 1)
                eng.memset(c.ones16[:, :], 1.0).then_inc(s_z.sem, 1)
                eng.wait_ge(*s_const(48))
                eng.tensor_copy(c.before16[:, :], stage[:, 0, 0:P]).then_inc(s_z.sem, 1)
                eng.wait_ge(*s_z(3))
                c.dve_link = Chain(eng, s_link.sem)
                for g in progs:
                    if "dve" in g:
                        g["dve"](eng)

            @block.tensor
            def _(eng):
                eng.wait_ge(*s_z(3))
                eng.wait_ge(*s_const(48))
                for g in progs:
                    if "pe" in g:
                        g["pe"](eng)

            @block.gpsimd
            def _(eng):
                for g in progs:
                    if "pool" in g:
                        g["pool"](eng)


def layouts(v):
    import numpy as np
    f = lambda a: np.ascontiguousarray(a, dtype=np.float32) if a.dtype == np.float32 else np.ascontiguousarray(a)
    v = {k: np.asarray(a) for k, a in v.items()}
    io = np.concatenate([np.tile(np.arange(E0), NT), np.tile(np.arange(E1), NT), np.arange(32), np.arange(NT) * P])
    j = np.arange(P)
    d = dict(
        x=v["L0_attn_x"].reshape(T, D),
        gate=v["L0_ffn_gate_w"].reshape(E0, KD, P).transpose(2, 1, 0).reshape(P, KD * E0),
        w_gate=v["L0_ffn_w_gate"].reshape(E0, FF, KD, P).transpose(3, 0, 2, 1).reshape(P, -1),
        w_up=v["L0_ffn_w_up"].reshape(E0, FF, KD, P).transpose(3, 0, 2, 1).reshape(P, -1),
        w_down=v["L0_ffn_w_down"].reshape(E0, D, CF, P).transpose(3, 0, 2, 1).reshape(P, -1),
        rw1=v["L1_ffn_rw1"].reshape(KD, P, P).transpose(1, 0, 2).reshape(P, -1),
        rw2=v["L1_ffn_rw2"],
        w1=v["L1_ffn_w1"].reshape(E1, KD, P, FF).transpose(2, 0, 1, 3).reshape(P, -1),
        w2=v["L1_ffn_w2"].reshape(E1, CF, P, D).transpose(2, 0, 1, 3).reshape(P, -1),
        b1row=v["L1_ffn_b1"],
        b1col=v["L1_ffn_b1"].reshape(E1, CF, P).transpose(2, 0, 1).reshape(P, -1),
        b2=v["L1_ffn_b2"],
        ident=np.eye(P, dtype=np.float32),
        before=(j[:, None] < j[None, :]).astype(np.float32),
        iota=np.concatenate([np.tile(io, (P, 1)), (j % E1)[:, None]], 1).astype(np.float32),
    )
    d.update(attention_layouts(v))
    d.update(mixer_layouts(v))
    return {k: f(a) for k, a in d.items()}


def build(nc, arrays, stages="fafmsm"):
    A = {k: nc.dram_tensor(f"in_{k}", a.shape, mybir.dt.from_np(a.dtype), kind="ExternalInput").ap() for k, a in arrays.items()}
    scratch = dict(xg_dram=(NB1 * P, D, F32), yg_dram=(NB1 * P, D, F32), **attention_scratch())
    for k, (*shape, dt) in scratch.items():
        A[k] = nc.dram_tensor(k, tuple(shape), dt, kind="Internal").ap()
    out = nc.dram_tensor("out_x", (T, D), F32, kind="ExternalOutput").ap()
    program(nc, A, out, stages)


def kernel(**inputs):
    import concourse.bacc as _bacc
    from concourse.bass_utils import run_bass_kernel_spmd as _run

    nc = _bacc.Bacc("TRN2", target_bir_lowering=False, num_devices=1)
    arrays = layouts(inputs)
    build(nc, arrays)
    r = _run(nc, [{f"in_{k}": a for k, a in arrays.items()}], core_ids=[0])
    return r.results[0]["out_x"].reshape(1, T, D)
```
